# Optimizing a Trainium2 kernel written in Bass

```python
import numpy as np
import jax
import jax.numpy as jnp

def _softmax(x, axis=-1):
    return jax.nn.softmax(x, axis=axis)

def _gelu(x):
    return jax.nn.gelu(x, approximate=True)

def _silu(x):
    return jax.nn.silu(x)

def _sigmoid(x):
    return jax.nn.sigmoid(x)

def _layernorm(x, axis=-1, eps=1e-05):
    m = jnp.mean(x, axis=axis, keepdims=True)
    v = jnp.var(x, axis=axis, keepdims=True)
    return (x - m) / jnp.sqrt(v + eps)

def _scatter_add(tgt, idx, src, axis=0):
    return tgt.at[idx].add(src)

def _segment_sum(src, seg, n):
    return jax.ops.segment_sum(src, seg, n)
kernel_name = 'mk_conv_seq_d2_conv_nchw512_r4_c5bf84'

def setup_inputs(seed: int=0):
    np.random.seed(seed)
    _w = jnp.asarray

    def _rec_inputs():
        import jax
        import jax.numpy as jnp
        _gk = jax.random.key(seed)
        x = -7.109e-05 + 0.9999 * jax.random.normal(jax.random.fold_in(_gk, 1), (8, 128, 32, 32), jnp.float32)
        return x
    x = _rec_inputs()

    def _L0_conv_setup():
        import jax, jax.numpy as jnp
        import numpy as np
        EPS = 1e-05
        WIN = 8
        HEADS = 8

        def _layernorm(x, g, b):
            mu = jnp.mean(x, axis=-1, keepdims=True)
            var = jnp.mean(jnp.square(x - mu), axis=-1, keepdims=True)
            return (x - mu) * jax.lax.rsqrt(var + EPS) * g + b
        key = jax.random.key(seed)
        ks = jax.random.split(key, 8)
        B, C, H, W = (8, 128, 32, 32)
        hidden = int(C * 2.0)
        s = 0.02
        return {'x': jax.random.normal(ks[0], (B, C, H, W), jnp.float32), 'ln1_g': jnp.ones((C,), jnp.float32), 'ln1_b': jnp.zeros((C,), jnp.float32), 'in_w': jax.random.normal(ks[1], (3 * C, C), jnp.float32) * s, 'in_b': jnp.zeros((3 * C,), jnp.float32), 'out_w': jax.random.normal(ks[2], (C, C), jnp.float32) * s, 'out_b': jnp.zeros((C,), jnp.float32), 'ln2_g': jnp.ones((C,), jnp.float32), 'ln2_b': jnp.zeros((C,), jnp.float32), 'fc1_w': jax.random.normal(ks[3], (hidden, C), jnp.float32) * s, 'fc1_b': jnp.zeros((hidden,), jnp.float32), 'fc2_w': jax.random.normal(ks[4], (C, hidden), jnp.float32) * s, 'fc2_b': jnp.zeros((C,), jnp.float32)}
    _L0_conv_all = _L0_conv_setup()
    _L0_conv_in = {k: v for k, v in _L0_conv_all.items() if k in ('ln1_g', 'ln1_b', 'in_w', 'in_b', 'out_w', 'out_b', 'ln2_g', 'ln2_b', 'fc1_w', 'fc1_b', 'fc2_w', 'fc2_b')}
    del _L0_conv_all

    def _L1_conv_setup():
        import jax, jax.numpy as jnp
        import numpy as np
        key = jax.random.key(seed)
        ks = jax.random.split(key, 9)
        B, C, H, W = (8, 128, 56, 56)
        E = 64
        s = 0.02
        return {'x': jax.random.normal(ks[0], (B, C, H, W), dtype=jnp.float32), 'wq': jax.random.normal(ks[1], (E, C), dtype=jnp.float32) * s, 'bq': jax.random.normal(ks[2], (E,), dtype=jnp.float32) * s, 'wk': jax.random.normal(ks[3], (E, C), dtype=jnp.float32) * s, 'bk': jax.random.normal(ks[4], (E,), dtype=jnp.float32) * s, 'wv': jax.random.normal(ks[5], (E, C), dtype=jnp.float32) * s, 'bv': jax.random.normal(ks[6], (E,), dtype=jnp.float32) * s, 'wo': jax.random.normal(ks[7], (C, E), dtype=jnp.float32) * s, 'bo': jax.random.normal(ks[8], (C,), dtype=jnp.float32) * s}
    _L1_conv_all = _L1_conv_setup()
    _L1_conv_in = {k: v for k, v in _L1_conv_all.items() if k in ('wq', 'bq', 'wk', 'bk', 'wv', 'bv', 'wo', 'bo')}
    del _L1_conv_all
    return {'x': x, 'L0_conv_ln1_g': _L0_conv_in['ln1_g'], 'L0_conv_ln1_b': _L0_conv_in['ln1_b'], 'L0_conv_in_w': _L0_conv_in['in_w'], 'L0_conv_in_b': _L0_conv_in['in_b'], 'L0_conv_out_w': _L0_conv_in['out_w'], 'L0_conv_out_b': _L0_conv_in['out_b'], 'L0_conv_ln2_g': _L0_conv_in['ln2_g'], 'L0_conv_ln2_b': _L0_conv_in['ln2_b'], 'L0_conv_fc1_w': _L0_conv_in['fc1_w'], 'L0_conv_fc1_b': _L0_conv_in['fc1_b'], 'L0_conv_fc2_w': _L0_conv_in['fc2_w'], 'L0_conv_fc2_b': _L0_conv_in['fc2_b'], 'L1_conv_wq': _L1_conv_in['wq'], 'L1_conv_bq': _L1_conv_in['bq'], 'L1_conv_wk': _L1_conv_in['wk'], 'L1_conv_bk': _L1_conv_in['bk'], 'L1_conv_wv': _L1_conv_in['wv'], 'L1_conv_bv': _L1_conv_in['bv'], 'L1_conv_wo': _L1_conv_in['wo'], 'L1_conv_bo': _L1_conv_in['bo']}

def reference(x, L0_conv_ln1_g, L0_conv_ln1_b, L0_conv_in_w, L0_conv_in_b, L0_conv_out_w, L0_conv_out_b, L0_conv_ln2_g, L0_conv_ln2_b, L0_conv_fc1_w, L0_conv_fc1_b, L0_conv_fc2_w, L0_conv_fc2_b, L1_conv_wq, L1_conv_bq, L1_conv_wk, L1_conv_bk, L1_conv_wv, L1_conv_bv, L1_conv_wo, L1_conv_bo):
    import jax
    import jax.numpy as jnp

    def _L0_conv_ref(x, ln1_g, ln1_b, in_w, in_b, out_w, out_b, ln2_g, ln2_b, fc1_w, fc1_b, fc2_w, fc2_b):
        import jax, jax.numpy as jnp
        import numpy as np
        EPS = 1e-05
        WIN = 8
        HEADS = 8

        def _layernorm(x, g, b):
            mu = jnp.mean(x, axis=-1, keepdims=True)
            var = jnp.mean(jnp.square(x - mu), axis=-1, keepdims=True)
            return (x - mu) * jax.lax.rsqrt(var + EPS) * g + b
        B, C, H, W = x.shape
        w = WIN
        nH, nW = (H // w, W // w)
        S = w * w
        dh = C // HEADS
        win = x.reshape(B, C, nH, w, nW, w).transpose(0, 2, 4, 3, 5, 1).reshape(B * nH * nW, S, C)
        normed = _layernorm(win, ln1_g, ln1_b)
        qkv = normed @ in_w.T + in_b
        q, k, v = jnp.split(qkv, 3, axis=-1)

        def heads(t):
            return t.reshape(-1, S, HEADS, dh).transpose(0, 2, 1, 3)
        q, k, v = (heads(q), heads(k), heads(v))
        scores = jnp.einsum('bhsd,bhtd->bhst', q, k) / jnp.sqrt(jnp.float32(dh))
        attn = jax.nn.softmax(scores, axis=-1)
        o = jnp.einsum('bhst,bhtd->bhsd', attn, v).transpose(0, 2, 1, 3).reshape(-1, S, C)
        o = o @ out_w.T + out_b
        win = win + o
        y = win.reshape(B, nH, nW, w, w, C).transpose(0, 5, 1, 3, 2, 4).reshape(B, C, H, W)
        y = y.transpose(0, 2, 3, 1)
        h = _layernorm(y, ln2_g, ln2_b)
        h = jax.nn.silu(h @ fc1_w.T + fc1_b) @ fc2_w.T + fc2_b
        y = y + h
        return y.transpose(0, 3, 1, 2)

    def _L1_conv_ref(x, wq, bq, wk, bk, wv, bv, wo, bo):
        import jax, jax.numpy as jnp
        import numpy as np
        B, C, H, W = x.shape
        N = H * W
        xf = x.reshape(B, C, N)
        q = jnp.einsum('ec,bcn->bne', wq, xf) + bq
        k = jnp.einsum('ec,bcn->ben', wk, xf) + bk[None, :, None]
        v = jnp.einsum('ec,bcn->bne', wv, xf) + bv
        attn = jnp.einsum('bne,bem->bnm', q, k) / N
        embed = jnp.einsum('bnm,bme->bne', attn, v)
        out = jnp.einsum('ce,bne->bcn', wo, embed) + bo[None, :, None]
        return out.reshape(B, C, H, W) + x

    def _gn(v, G=32, eps=1e-05):
        B_, C_, H_, W_ = v.shape
        g = v.reshape(B_, G, C_ // G, H_, W_)
        m = jnp.mean(g, axis=(2, 3, 4), keepdims=True)
        s = jnp.var(g, axis=(2, 3, 4), keepdims=True)
        return ((g - m) / jnp.sqrt(s + eps)).reshape(v.shape)

    def _ln_c(v, eps=1e-06):
        m = jnp.mean(v, axis=1, keepdims=True)
        s = jnp.var(v, axis=1, keepdims=True)
        return (v - m) / jnp.sqrt(s + eps)

    def _ln_t(v, eps=1e-05):
        m = jnp.mean(v, axis=-1, keepdims=True)
        s = jnp.var(v, axis=-1, keepdims=True)
        return (v - m) / jnp.sqrt(s + eps)

    def _to_tokens(v):
        B_, C_, H_, W_ = v.shape
        return v.reshape(B_, C_, H_ * W_).transpose(0, 2, 1)

    def _from_tokens(t, like):
        B_, C_, H_, W_ = like.shape
        return t.transpose(0, 2, 1).reshape(B_, C_, H_, W_)
    x = _L0_conv_ref(x, L0_conv_ln1_g, L0_conv_ln1_b, L0_conv_in_w, L0_conv_in_b, L0_conv_out_w, L0_conv_out_b, L0_conv_ln2_g, L0_conv_ln2_b, L0_conv_fc1_w, L0_conv_fc1_b, L0_conv_fc2_w, L0_conv_fc2_b)
    x = _L1_conv_ref(x, L1_conv_wq, L1_conv_bq, L1_conv_wk, L1_conv_bk, L1_conv_wv, L1_conv_bv, L1_conv_wo, L1_conv_bo)
    return x

_drawn_inputs = setup_inputs


def setup_inputs(seed=0):
    import zlib

    import numpy as np

    out = dict(_drawn_inputs(seed))
    spreads = {'L0_conv_ln1_g': (1.0, 0.6),
     'L0_conv_ln1_b': (0.0, 0.8),
     'L0_conv_in_b': (0.0, 0.356),
     'L0_conv_out_b': (0.0, 0.1),
     'L0_conv_ln2_g': (1.0, 0.6),
     'L0_conv_ln2_b': (0.0, 0.8),
     'L0_conv_fc1_b': (0.0, 0.457),
     'L0_conv_fc2_b': (0.0, 0.1)}
    factors = {'L0_conv_in_w': 6.692,
     'L1_conv_wq': 8.0,
     'L1_conv_bq': 8.0,
     'L1_conv_wk': 8.0,
     'L1_conv_bk': 8.0,
     'L1_conv_wv': 8.0,
     'L1_conv_bv': 8.0,
     'L1_conv_wo': 8.0,
     'L1_conv_bo': 21.832}
    for name, (base, spread) in spreads.items():
        noise = np.random.default_rng([zlib.crc32(name.encode()), seed]).standard_normal(out[name].shape)
        drawn = base * np.exp(spread * noise) if base else spread * noise
        out[name] = jnp.asarray(drawn.astype(out[name].dtype))
    for name, factor in factors.items():
        out[name] = (out[name] * factor).astype(out[name].dtype)
    return out
```

```python
from contextlib import ExitStack

import concourse.bass as bass
from concourse import mybir

F32 = mybir.dt.float32
F32R = mybir.dt.float32r
BF16 = mybir.dt.bfloat16
ACT = mybir.ActivationFunctionType
ALU = mybir.AluOpType
AXIS_X = mybir.AxisListType.X

IMAGES, C, SIDE = 8, 128, 32
WIN = 8
KEYS = WIN * WIN
TOKENS = SIDE * SIDE
HALF = TOKENS // 2
WH = HALF // KEYS
PAIRS = WH // 2
HEADS, DH = 8, 16
QUADS = 4
HIDDEN = 256
E = 64
EPS = 1e-5
SCORE_SCALE = DH ** -0.5
VB = DH + 1
Q_, K_, O_, F1_, F2_ = 0, 1, 2, 3, 5


class Loop:

    def __init__(self, eng, i):
        self.eng, self.i, self.kept = eng, i, {}

    def number(self, a, b):
        if isinstance(self.i, int):
            return a * self.i + b
        if (a, b) not in self.kept:
            self.kept[a, b] = self.eng.snap(self.i * a + b)
        return self.kept[a, b]

    def half(self, c):
        return Half(self, c)

    def image(self, c, times=1):
        return self.number(times, times * (c + 1))

    def follows(self, c):
        return not isinstance(self.i, int) or self.i + c >= 0


class Half:

    def __init__(self, loop, c):
        self.loop, self.c, self.par = loop, c, c % 2

    def n(self, back=0, times=1):
        return self.loop.number(2 * times, times * (self.c - back + 1))

    def of_parity(self, back=0, times=1):
        return self.loop.number(times, times * ((self.c - back) // 2 + 1))

    def follows(self, back):
        return not isinstance(self.loop.i, int) or 2 * self.loop.i + self.c - back >= 0


def build(nc, x, ln1_g, ln1_b, in_w, in_b, out_w, out_b, ln2_g, ln2_b, fc1_w, fc1_b, fc2_w, fc2_b,
          wq, bq, wk, bk, wv, bv, wo, bo, out):
    ctx = ExitStack()
    with ctx:
        def sb(name, shape, dt=F32):
            return ctx.enter_context(nc.sbuf_tensor(name, shape, dt))

        def sem(name):
            return ctx.enter_context(nc.semaphore(name))

        def sems(name, n):
            return [sem(f"{name}{k}") for k in range(n)]

        in_w_rows = sb("in_w_rows", [128, 3, C])
        out_w_rows = sb("out_w_rows", [128, C])
        fc1_rows = sb("fc1_rows", [128, 2, C])
        fc2_rows = sb("fc2_rows", [128, HIDDEN])
        kv_rows = sb("kv_rows", [2 * E, C])
        wo_rows = sb("wo_rows", [C, E])
        wq_rows = sb("wq_rows", [E, C])
        cols = sb("cols", [128, 16])
        G1, B1, G2, B2, INB, OUTB, FC1B, FC2B, BO, BQ = 0, 1, 2, 3, 4, 7, 8, 10, 11, 12
        kv_bias = sb("kv_bias", [128, 2 * E])
        wT = sb("wT", [128, 10, C])
        w_full = sb("w_full", [128, 7, C])
        wh = sb("wh", [128, 7, C], F32R)
        wl = sb("wl", [128, 7, C], F32R)
        wv_cols = sb("wv_cols", [128, C])
        qkv_b = sb("qkv_b", [128, 3])
        fc1_b2 = sb("fc1_b2", [128, 2])
        out_b2 = sb("out_b2", [128, 1])
        head_a = sb("head_a", [128, 2])
        ident = sb("ident", [128, 128])
        neg_ident = sb("neg_ident", [128, 128], BF16)
        minus_half = sb("minus_half", [128, 4])

        x_in = sb("x_in", [C, 2, HALF])
        x_win = sb("x_win", [C, HALF])
        x_res = sb("x_res", [C, 2, HALF])
        stats1 = sb("stats1", [128, 4, 6])
        mv1 = sb("mv1", [128, 4, 2])
        rstd1 = sb("rstd1", [128, 4])
        xn_tok = sb("xn_tok", [128, 4, C])
        xn = sb("xn", [C, HALF])
        xn_h = sb("xn_h", [C, HALF], F32R)
        xn_l = sb("xn_l", [C, HALF], F32R)
        q_h = sb("q_h", [C, HALF], F32R)
        q_l = sb("q_l", [C, HALF], F32R)
        k_h = sb("k_h", [C, HALF], F32R)
        k_l = sb("k_l", [C, HALF], F32R)
        v_tok = sb("v_tok", [128, PAIRS, C])
        qd_h = sb("qd_h", [C, 2, QUADS, HALF], F32R)
        qd_l = sb("qd_l", [C, 2, QUADS, HALF], F32R)
        kd_h = sb("kd_h", [C, 2, WH, 2, KEYS], F32R)
        kd_l = sb("kd_l", [C, 2, WH, 2, KEYS], F32R)
        vd = sb("vd", [128, 2, WH, 2, VB, QUADS])

        row_max = sb("row_max", [128, HEADS])
        max_wide = sb("max_wide", [128, 2, HEADS, KEYS], BF16)
        probs = sb("probs", [128, 2, 2, QUADS, KEYS])
        inv_sum = sb("inv_sum", [128, HEADS])
        o_tok = sb("o_tok", [128, PAIRS, C])

        o_h = sb("o_h", [C, HALF], F32R)
        o_l = sb("o_l", [C, HALF], F32R)
        y1 = sb("y1", [C, HALF])
        stats2 = sb("stats2", [128, 4, 6])
        mv2 = sb("mv2", [128, 4, 2])
        rstd2 = sb("rstd2", [128, 4])
        yn_tok = sb("yn_tok", [128, 4, C])
        yn_h = sb("yn_h", [C, HALF], F32R)
        yn_l = sb("yn_l", [C, HALF], F32R)
        hid = sb("hid", [128, 2, HALF])
        hid_h = sb("hid_h", [128, 2, HALF], F32R)
        hid_l = sb("hid_l", [128, 2, HALF], F32R)
        y2 = sb("y2", [C, HALF])
        y2_h = sb("y2_h", [C, 2, HALF], F32R)
        y2_l = sb("y2_l", [C, 2, HALF], F32R)
        kv_tok = sb("kv_tok", [128, 2, 4, 2 * E])

        kvT = sb("kvT", [E, E])
        bT = sb("bT", [E, C])
        mT = sb("mT", [C, C])
        m_h = sb("m_h", [C, C], F32R)
        m_l = sb("m_l", [C, C], F32R)
        d_col = sb("d_col", [C, 1])
        out_sb = sb("out_sb", [C, 2, HALF])

        def bank(name, dt=F32):
            return ctx.enter_context(nc.psum_tensor(name, [128, 512], dt))

        p_score = bank("p_score")
        p_scoreT = bank("p_scoreT")
        p_attn = bank("p_attn")
        p_a = [bank("p_a0"), bank("p_a1")]
        p_c = [bank("p_c0"), bank("p_c1")]
        p_d = bank("p_d")

        w_dma = sem("w_dma")
        const_set, ident_set, const_ready = sem("const_set"), sem("ident_set"), sem("const_ready")
        wT_ready, wT_kept, bias_ready, bias_kept = sem("wT_ready"), sem("wT_kept"), sem("bias_ready"), sem("bias_kept")
        ob_ready, ob_kept, w_scaled, w_high, w_ready = (
            sem("ob_ready"), sem("ob_kept"), sem("w_scaled"), sem("w_high"), sem("w_ready"))
        x_dma = sems("x_dma", 2)
        x_win_set, x_res_set = sem("x_win_set"), sem("x_res_set")
        xT_ready, ln1_stats, ln1_mv, ln1_var, ln1_rstd, xn_tok_set = (
            sem("xT_ready"), sem("ln1_stats"), sem("ln1_mv"), sem("ln1_var"), sem("ln1_rstd"), sem("xn_tok_set"))
        xnT_ready, xn_high, xn_low, xn_full = sem("xnT_ready"), sem("xn_high"), sem("xn_low"), sem("xn_full")
        q_ready, q_high, q_low, k_ready, k_high, k_low = (
            sem("q_ready"), sem("q_high"), sem("q_low"), sem("k_ready"), sem("k_high"), sem("k_low"))
        v_ready, v_kept = sem("v_ready"), sem("v_kept")
        q_dma, v_dma = sem("q_dma"), sem("v_dma")
        kd_ready = sem("kd_ready")
        score_ready, max_ready, max_wide_ready = sems("score_ready", 4), sems("max_ready", 4), sems("max_wide_ready", 4)
        scoreT_ready, probs_ready = sems("scoreT_ready", 4), sems("probs_ready", 4)
        attn_ready, inv_ready, o_tok_ready = sems("attn_ready", 4), sems("inv_ready", 4), sems("o_tok_ready", 4)
        oT_ready, o_high, o_low, proj_ready, y1_ready = (
            sem("oT_ready"), sem("o_high"), sem("o_low"), sem("proj_ready"), sem("y1_ready"))
        yT_ready, ln2_stats, ln2_mv, ln2_var, ln2_rstd, yn_tok_set = (
            sem("yT_ready"), sem("ln2_stats"), sem("ln2_mv"), sem("ln2_var"), sem("ln2_rstd"), sem("yn_tok_set"))
        ynT_ready, yn_high, yn_low = sem("ynT_ready"), sem("yn_high"), sem("yn_low")
        fc1_ready, hid_high, hid_full, hid_low = sems("fc1_ready", 2), sems("hid_high", 2), sems("hid_full", 2), sems("hid_low", 2)
        fc2_ready, y2_ready, y2_high, y2_low = sem("fc2_ready"), sem("y2_ready"), sem("y2_high"), sem("y2_low")
        kv_ready, kv_kept = sem("kv_ready"), sem("kv_kept")
        kvT_ready, kvT_kept, bT_ready, bT_kept = sem("kvT_ready"), sem("kvT_kept"), sem("bT_ready"), sem("bT_kept")
        mT_ready, mT_kept, m_high, m_low, d_kept = sem("mT_ready"), sem("mT_kept"), sem("m_high"), sem("m_low"), sem("d_kept")
        fin_ready, fin_kept = sems("fin_ready", 2), sems("fin_kept", 2)
        out_dma = sems("out_dma", 2)
        pool_waits, pe_waits, dve_waits = sem("pool_waits"), sem("pe_waits"), sem("dve_waits")

        W_LOADS = 20

        def col(k, n=1, rows=128):
            return cols[0:rows, k:k + n]

        def images(eng, prologue, step_even, step_odd, epilogue):
            prologue(Loop(eng, 0))
            first, last = Loop(eng, 0), Loop(eng, IMAGES - 1)
            step_even(first, more=True, c=False)
            step_odd(first, more=True, d=False)
            with eng.Fori(1, IMAGES - 1) as i:
                body = Loop(eng, i)
                step_even(body, more=True, c=True)
                step_odd(body, more=True, d=True)
            step_even(last, more=False, c=True)
            step_odd(last, more=False, d=True)
            epilogue(last)

        block = ctx.enter_context(nc.Block())

        @block.sync
        def _(sp):
            def load(dst, src):
                sp.dma_start(dst, src).then_inc(w_dma, 16)

            def column(v, n=1):
                return v.rearrange("(n p) -> p n", n=n)

            x_rows = x.rearrange("b c (h row) win -> b h c (row win)", h=2)

            def load_x(h):
                src = x_rows[h.loop.number(1, h.c // 2), h.par]
                if h.follows(2):
                    sp.wait_ge(x_win_set, h.n(2))
                if h.follows(2):
                    sp.wait_ge(x_res_set, h.n(2))
                sp.dma_start(x_in[:, h.par, :], src).then_inc(x_dma[h.par], 16)

            first = Loop(sp, 0)
            load_x(first.half(0))
            load(in_w_rows[:], in_w.rearrange("(n p) c -> p n c", n=3))
            load(out_w_rows[:], out_w)
            load(fc1_rows[:], fc1_w.rearrange("(n p) c -> p n c", n=2))
            load(fc2_rows[:], fc2_w)
            load(kv_rows[0:E, :], wk)
            load(kv_rows[E:2 * E, :], wv)
            load(wo_rows[:], wo)
            load(wq_rows[:], wq)
            with nc.allow_non_contiguous_dma(reason="biases and gains, one element per partition"):
                load(col(INB, 3), column(in_b, 3))
                load(col(FC1B, 2), column(fc1_b, 2))
                for k, v in ((G1, ln1_g), (B1, ln1_b), (G2, ln2_g), (B2, ln2_b), (OUTB, out_b),
                             (FC2B, fc2_b), (BO, bo)):
                    load(col(k), column(v))
                load(col(BQ, rows=E), column(bq))
            load(kv_bias[:, 0:E], bass.AP(bk.tensor, 0, [[0, 128], [1, E]]))
            load(kv_bias[:, E:2 * E], bass.AP(bv.tensor, 0, [[0, 128], [1, E]]))

            def spread_q(h):
                sp.wait_ge(q_high, h.n())
                if h.follows(2):
                    sp.wait_ge(scoreT_ready[PAIRS - 1], h.n(2))
                for j in range(QUADS):
                    head_pair = slice(32 * j, 32 * j + 32)
                    sp.dma_start(qd_h[head_pair, h.par, j, :].bitcast(F32), q_h[head_pair, :].bitcast(F32)).then_inc(q_dma, 16)
                sp.wait_ge(q_low, h.n())
                for j in range(QUADS):
                    head_pair = slice(32 * j, 32 * j + 32)
                    sp.dma_start(qd_l[head_pair, h.par, j, :].bitcast(F32), q_l[head_pair, :].bitcast(F32)).then_inc(q_dma, 16)

            def spread_v(h):
                sp.wait_ge(v_kept, h.n())
                if h.follows(2):
                    sp.wait_ge(attn_ready[PAIRS - 1], h.n(2))
                slot = vd[:, h.par].rearrange("row (p win) a d j -> row p win a (d j)", win=2)
                for a in range(2):
                    for win in range(2):
                        sp.dma_start(slot[64 * a:64 * a + 64, :, win, a, 0:KEYS],
                                     v_tok[64 * win:64 * win + 64, :, 64 * a:64 * a + 64]).then_inc(v_dma, 16)

            def store(loop, c):
                for half in range(2):
                    dst = out.rearrange("b c (h row) win -> b h c (row win)", h=2)[loop.number(1, c), half]
                    sp.wait_ge(fin_kept[half], loop.image(c))
                    sp.dma_start(dst, out_sb[:, half, :]).then_inc(out_dma[half], 16)

            def prologue(loop):
                sp.wait_ge(const_set, 7)
                spread_q(loop.half(0))
                spread_v(loop.half(0))
                load_x(loop.half(1))

            def step_even(loop, more, c):
                if more:
                    load_x(loop.half(2))
                spread_q(loop.half(1))
                spread_v(loop.half(1))

            def step_odd(loop, more, d):
                if more:
                    load_x(loop.half(3))
                    spread_q(loop.half(2))
                    spread_v(loop.half(2))
                if d:
                    store(loop, -1)

            def epilogue(loop):
                store(loop, 0)
                for half in range(2):
                    sp.wait_ge(out_dma[half], 16 * IMAGES)

            images(sp, prologue, step_even, step_odd, epilogue)


        @block.gpsimd
        def _(pool):
            pool.memset(ident[:], 0.0).then_inc(ident_set, 1)
            pool.wait_ge(ident_set, 1)
            pool.affine_select(out=ident[:], in_=ident[:], compare_op=ALU.not_equal, fill=1.0, base=0,
                               pattern=[[-1, 128]], channel_multiplier=1).then_inc(ident_set, 1)
            pool.wait_ge(ident_set, 2)
            pool.tensor_scalar(neg_ident[:], ident[:], -1.0, None, ALU.mult).then_inc(const_ready, 1)
            pool.memset(minus_half[:], -0.5).then_inc(const_ready, 1)

            def waited():
                pool.sem_inc(pool_waits, 1)

            def windows(h):
                return x_in[:, h.par, :].rearrange("p (v row win c) -> p v win row c", v=2, row=WIN, win=4)

            def order(h):
                pool.wait_ge(x_dma[h.par], h.of_parity(times=16))
                if h.follows(1):
                    pool.wait_ge(xT_ready, h.n(1))
                waited()
                dst = x_win[:].rearrange("p (v win row c) -> p v win row c", v=2, win=4, row=WIN)
                pool.tensor_copy(dst[:, 0], windows(h)[:, 0])
                pool.tensor_copy(dst[:, 1], windows(h)[:, 1]).then_inc(x_win_set, 1)

            def residual(h):
                if h.follows(2):
                    pool.wait_ge(y1_ready, h.n(2))
                waited()
                dst = x_res[:, h.par, :].rearrange("p (v win row c) -> p v win row c", v=2, win=4, row=WIN)
                pool.tensor_scalar(dst[:, 0], windows(h)[:, 0], out_b2[:, 0:1], None, ALU.add)
                pool.tensor_scalar(dst[:, 1], windows(h)[:, 1], out_b2[:, 0:1], None, ALU.add).then_inc(x_res_set, 1)

            def rstd(h, mv, mv_set, var_set, out_, out_set, read):
                pool.wait_ge(mv_set, h.n())
                if h.follows(1):
                    pool.wait_ge(read, h.n(1))
                waited()
                pool.tensor_scalar(out_[:], mv[:, :, 1], EPS, None, ALU.add).then_inc(var_set, 1)
                pool.wait_ge(var_set, h.n())
                pool.tensor_tensor(out_[:], out_[:], minus_half[:], ALU.pow).then_inc(out_set, 1)

            def spread_k(h):
                if h.follows(2):
                    pool.wait_ge(scoreT_ready[PAIRS - 1], h.n(2))
                for src, dst, ready in ((k_h, kd_h, k_high), (k_l, kd_l, k_low)):
                    pool.wait_ge(ready, h.n())
                    waited()
                    for a in range(2):
                        last = pool.tensor_scalar(dst[:, h.par, :, a, :],
                                                  src[:].bitcast(F32).rearrange("p (win k) -> p win k", k=KEYS),
                                                  head_a[:, a:a + 1], None, ALU.mult)
                last.then_inc(kd_ready, 1)

            def widen(h, p):
                pool.wait_ge(max_ready[p], h.n())
                if p < 2:
                    if h.follows(1):
                        pool.wait_ge(scoreT_ready[p + 2], h.n(1))
                else:
                    pool.wait_ge(scoreT_ready[p - 2], h.n())
                waited()
                pool.tensor_copy(max_wide[:, p % 2], row_max[:].unsqueeze(2).to_broadcast([128, HEADS, KEYS])
                                 ).then_inc(max_wide_ready[p], 1)

            def hidden_low(h, t):
                pool.wait_ge(hid_high[t], h.n())
                pool.wait_ge(hid_full[t], h.n())
                if h.follows(1):
                    pool.wait_ge(fc2_ready, h.n(1))
                pool.tensor_tensor(hid_l[:, t], hid[:, t], hid_h[:, t].bitcast(F32), ALU.subtract).then_inc(hid_low[t], 1)

            def y2_split(h):
                pool.wait_ge(y2_ready, h.n())
                if h.follows(2):
                    pool.wait_ge(fin_ready[h.par], h.of_parity(2))
                waited()
                pool.tensor_copy(y2_h[:, h.par], y2[:]).then_inc(y2_high, 1)
                pool.wait_ge(y2_high, h.n())
                pool.tensor_tensor(y2_l[:, h.par], y2[:], y2_h[:, h.par].bitcast(F32), ALU.subtract).then_inc(y2_low, 1)

            def rstd1_of(h):
                rstd(h, mv1, ln1_mv, ln1_var, rstd1, ln1_rstd, xn_tok_set)

            def rstd2_of(h):
                rstd(h, mv2, ln2_mv, ln2_var, rstd2, ln2_rstd, yn_tok_set)

            def prologue(loop):
                a = loop.half(0)
                order(a)
                rstd1_of(a)
                pool.wait_ge(ob_kept, 1)
                residual(a)
                spread_k(a)

            def step(loop, b, with_a, with_c):
                a, c = loop.half(b.c + 1), loop.half(b.c - 1)
                if with_a:
                    order(a)
                widen(b, 0)
                if with_a:
                    rstd1_of(a)
                widen(b, 1)
                if with_a:
                    residual(a)
                if with_c:
                    rstd2_of(c)
                widen(b, 2)
                if with_a:
                    spread_k(a)
                widen(b, 3)
                if with_c:
                    hidden_low(c, 0)
                    hidden_low(c, 1)
                    y2_split(c)

            def step_even(loop, more, c):
                step(loop, loop.half(0), True, c)

            def step_odd(loop, more, d):
                step(loop, loop.half(1), more, True)

            def epilogue(loop):
                c = loop.half(1)
                rstd2_of(c)
                hidden_low(c, 0)
                hidden_low(c, 1)
                y2_split(c)

            images(pool, prologue, step_even, step_odd, epilogue)

        @block.tensor
        def _(pe):
            def three_passes(dst, blocks, moving):
                passes = [(weight, moving_part) for (b_h, b_l), (m_h, m_l) in zip(blocks, moving)
                          for weight, moving_part in ((b_h, m_h), (b_h, m_l), (b_l, m_h))]
                for k, (weight, moving_part) in enumerate(passes):
                    last = pe.matmul(dst, weight, moving_part, start=k == 0, stop=k == len(passes) - 1)
                return last

            def weights(b):
                return wh[:, b, :], wl[:, b, :]

            def load_weights():
                pe.wait_ge(w_dma, 16 * W_LOADS)
                pe.wait_ge(ident_set, 2)
                blocks = [in_w_rows[:, k, :] for k in range(3)] + [out_w_rows[:]] + \
                         [fc1_rows[:, k, :] for k in range(2)] + [fc2_rows[:, 0:C], fc2_rows[:, C:2 * C]] + [kv_rows[:]]
                banks = [p_score, p_scoreT, p_attn]
                for k, weight in enumerate(blocks):
                    pe.transpose(banks[k // 4][:, C * (k % 4):C * (k % 4) + C], weight, ident[:])
                pe.transpose(p_attn[0:E, C:2 * C], wo_rows[:], ident[:]).then_inc(wT_ready, 1)
                pe.wait_ge(wT_kept, 1)
                for k, (b, v) in enumerate(((0, B1), (1, B1), (2, B1), (4, B2), (5, B2))):
                    last = pe.matmul(p_d[:, k:k + 1], wT[:, b, :], col(v), start=True, stop=True)
                last.then_inc(bias_ready, 1)
                pe.wait_ge(bias_kept, 1)
                pe.matmul(p_d[:, 8:9], wT[:, 3, :], qkv_b[:, 2:3], start=True, stop=True).then_inc(ob_ready, 1)

            def a_transpose(h):
                pe.wait_ge(x_win_set, h.n())
                if h.follows(1):
                    pe.wait_ge(v_kept, h.n(1))
                for t in range(4):
                    last = pe.transpose(p_a[0][:, C * t:C * t + C], x_win[:, C * t:C * t + C], ident[:])
                last.then_inc(xT_ready, 1)

            def a_back(h):
                pe.wait_ge(xn_tok_set, h.n())
                if h.follows(1):
                    pe.wait_ge(k_high, h.n(1))
                if h.follows(1):
                    pe.wait_ge(k_low, h.n(1))
                for t in range(4):
                    last = pe.transpose(p_a[1][:, C * t:C * t + C], xn_tok[:, t, :], ident[:])
                last.then_inc(xnT_ready, 1)

            def a_q(h):
                pe.wait_ge(xn_high, h.n())
                pe.wait_ge(xn_low, h.n())
                three_passes(p_a[0][:], [weights(Q_)], [(xn_h[:], xn_l[:])]).then_inc(q_ready, 1)

            def a_k(h):
                pe.wait_ge(xn_full, h.n())
                three_passes(p_a[1][:], [weights(K_)], [(xn_h[:], xn_l[:])]).then_inc(k_ready, 1)

            def a_v(h):
                pe.wait_ge(q_high, h.n())
                pe.wait_ge(q_low, h.n())
                for p in range(PAIRS):
                    last = pe.matmul(p_a[0][:, C * p:C * p + C], xn[:, C * p:C * p + C], wv_cols[:],
                                     start=True, stop=True)
                last.then_inc(v_ready, 1)

            def b_score(h, p):
                if p == 0:
                    pe.wait_ge(q_dma, h.n(times=16 * 2 * QUADS))
                    pe.wait_ge(kd_ready, h.n())
                    if h.follows(1):
                        pe.wait_ge(max_ready[PAIRS - 1], h.n(1))
                else:
                    pe.wait_ge(max_ready[p - 1], h.n())
                for j in range(QUADS):
                    for win, rows in ((1, 2 * KEYS), (0, KEYS)):
                        last = pe.matmul(p_score[0:rows, 2 * KEYS * j:2 * KEYS * (j + 1)],
                                         qd_h[:, h.par, j, 2 * KEYS * p:2 * KEYS * p + rows],
                                         kd_h[:, h.par, 2 * p + win], start=True, stop=True)
                last.then_inc(score_ready[p], 1)

            def b_scoreT(h, p):
                pe.wait_ge(max_wide_ready[p], h.n())
                if p == 0:
                    if h.follows(1):
                        pe.wait_ge(probs_ready[PAIRS - 1], h.n(1))
                else:
                    pe.wait_ge(probs_ready[p - 1], h.n())
                dst = p_scoreT[:].rearrange("row (win j q) -> row win j q", win=2, j=QUADS)
                for j in range(QUADS):
                    pe.matmul(dst[:, :, j, :], max_wide[:, p % 2, 2 * j:2 * j + 2, :],
                              neg_ident[:], start=j == 0, stop=False, skip_group_check=True)
                for win in range(2):
                    window = 2 * p + win
                    for k, (kd, qd) in enumerate(((kd_h, qd_h), (kd_h, qd_l), (kd_l, qd_h))):
                        last = pe.matmul(dst[:, win], kd[:, h.par, window], qd[:, h.par, :, KEYS * window:KEYS * (window + 1)],
                                         start=False, stop=win == 1 and k == 2, skip_group_check=True)
                last.then_inc(scoreT_ready[p], 1)

            def b_attn(h, p):
                pe.wait_ge(probs_ready[p], h.n())
                if p == 0:
                    pe.wait_ge(v_dma, h.n(times=16 * 4))
                    if h.follows(1):
                        pe.wait_ge(o_tok_ready[PAIRS - 1], h.n(1))
                else:
                    pe.wait_ge(o_tok_ready[p - 1], h.n())
                for win in range(2):
                    for j in range(QUADS):
                        last = pe.matmul(p_attn[64 * win:64 * win + 64, 2 * VB * j:2 * VB * (j + 1)],
                                         probs[:, p % 2, win, j, :],
                                         vd[:, h.par, 2 * p + win, :, :, j].rearrange("row a d -> row (a d)"),
                                         start=True, stop=True)
                last.then_inc(attn_ready[p], 1)

            def c_transpose(h):
                pe.wait_ge(o_tok_ready[PAIRS - 1], h.n())
                if h.follows(1):
                    pe.wait_ge(y2_ready, h.n(1))
                for p in range(PAIRS):
                    last = pe.transpose(p_c[0][:, C * p:C * p + C], o_tok[:, p, :], ident[:])
                last.then_inc(oT_ready, 1)

            def c_project(h):
                pe.wait_ge(o_high, h.n())
                pe.wait_ge(o_low, h.n())
                if h.follows(1):
                    pe.wait_ge(kv_kept, h.n(1))
                three_passes(p_c[1][:], [weights(O_)], [(o_h[:], o_l[:])]).then_inc(proj_ready, 1)

            def c_yT(h):
                pe.wait_ge(y1_ready, h.n())
                for t in range(4):
                    last = pe.transpose(p_c[0][:, C * t:C * t + C], y1[:, C * t:C * t + C], ident[:])
                last.then_inc(yT_ready, 1)

            def c_back(h):
                pe.wait_ge(yn_tok_set, h.n())
                for t in range(4):
                    last = pe.transpose(p_c[1][:, C * t:C * t + C], yn_tok[:, t, :], ident[:])
                last.then_inc(ynT_ready, 1)

            def c_fc1(h, t):
                pe.wait_ge(yn_high, h.n())
                pe.wait_ge(yn_low, h.n())
                three_passes(p_c[t][:], [weights(F1_ + t)], [(yn_h[:], yn_l[:])]).then_inc(fc1_ready[t], 1)

            def c_fc2(h):
                pe.wait_ge(hid_high[0], h.n())
                pe.wait_ge(hid_low[0], h.n())
                pe.wait_ge(hid_high[1], h.n())
                pe.wait_ge(hid_low[1], h.n())
                three_passes(p_c[0][:], [weights(F2_), weights(F2_ + 1)],
                             [(hid_h[:, t], hid_l[:, t]) for t in range(2)]).then_inc(fc2_ready, 1)

            def c_kv(h):
                pe.wait_ge(y2_ready, h.n())
                for t in range(4):
                    last = pe.matmul(p_c[1][:, C * t:C * t + C], y2[:, C * t:C * t + C], wT[:, 8, :],
                                     start=True, stop=True)
                last.then_inc(kv_ready, 1)

            def d_kvT(loop, c):
                pe.wait_ge(kv_kept, loop.number(2, 2 * c + 2))
                if loop.follows(c - 1):
                    pe.wait_ge(fin_kept[1], loop.image(c - 1))
                for n in range(8):
                    tile = kv_tok[:, n // 4, n % 4]
                    last = pe.matmul(p_d[0:E, 0:E], tile[:, E:2 * E], tile[:, 0:E], start=n == 0, stop=n == 7)
                last.then_inc(kvT_ready, 1)

            def d_bT(loop, c):
                pe.wait_ge(kvT_kept, loop.image(c))
                pe.sem_inc(pe_waits, 1)
                pe.matmul(p_d[0:E, 0:C], kvT[:], wT[0:E, 9, :], start=True, stop=True).then_inc(bT_ready, 1)

            def d_mT(loop, c):
                pe.wait_ge(bT_kept, loop.image(c))
                pe.matmul(p_d[:, 0:C], wq_rows[:], bT[:], start=True, stop=True)
                pe.matmul(p_d[:, C:C + 1], bT[:], col(BQ, rows=E), start=True, stop=True).then_inc(mT_ready, 1)

            def d_final(loop, c, half):
                if half == 0:
                    pe.wait_ge(m_high, loop.image(c))
                    pe.wait_ge(m_low, loop.image(c))
                    pe.wait_ge(d_kept, loop.image(c))
                    pe.wait_ge(y2_low, loop.number(2, 2 * c + 2))
                else:
                    pe.wait_ge(fin_kept[0], loop.image(c))
                three_passes(p_d[:], [(m_h[:], m_l[:])], [(y2_h[:, half], y2_l[:, half])]).then_inc(fin_ready[half], 1)

            def prologue(loop):
                a = loop.half(0)
                pe.wait_ge(ident_set, 2)
                a_transpose(a)
                load_weights()
                a_back(a)
                pe.wait_ge(w_ready, 1)
                a_q(a)
                a_k(a)
                a_v(a)

            def step(loop, b, with_a, with_c, with_d):
                a, c = loop.half(b.c + 1), loop.half(b.c - 1)
                b_score(b, 0)
                if with_a:
                    a_transpose(a)
                if with_c:
                    c_transpose(c)
                if with_d:
                    d_kvT(loop, -1)
                b_scoreT(b, 0)
                b_score(b, 1)
                if with_c:
                    c_project(c)
                if with_d:
                    d_bT(loop, -1)
                if with_a:
                    a_back(a)
                b_attn(b, 0)
                b_scoreT(b, 1)
                b_score(b, 2)
                if with_c:
                    c_yT(c)
                if with_a:
                    a_q(a)
                if with_d:
                    d_mT(loop, -1)
                b_attn(b, 1)
                if with_a:
                    a_k(a)
                b_scoreT(b, 2)
                b_score(b, 3)
                if with_a:
                    a_v(a)
                if with_c:
                    c_back(c)
                if with_d:
                    d_final(loop, -1, 0)
                b_attn(b, 2)
                b_scoreT(b, 3)
                if with_c:
                    c_fc1(c, 0)
                    c_fc1(c, 1)
                if with_d:
                    d_final(loop, -1, 1)
                b_attn(b, 3)
                if with_c:
                    c_fc2(c)
                    c_kv(c)

            def step_even(loop, more, c):
                step(loop, loop.half(0), True, c, False)

            def step_odd(loop, more, d):
                step(loop, loop.half(1), more, True, d)

            def epilogue(loop):
                c = loop.half(1)
                c_transpose(c)
                c_project(c)
                c_yT(c)
                c_back(c)
                c_fc1(c, 0)
                c_fc1(c, 1)
                c_fc2(c)
                c_kv(c)
                d_kvT(loop, 0)
                d_bT(loop, 0)
                d_mT(loop, 0)
                d_final(loop, 0, 0)
                d_final(loop, 0, 1)

            images(pe, prologue, step_even, step_odd, epilogue)

        @block.scalar
        def _(act):
            def a_xn(h):
                act.wait_ge(xnT_ready, h.n())
                if h.follows(1):
                    act.wait_ge(q_ready, h.n(1))
                if h.follows(1):
                    act.wait_ge(v_ready, h.n(1))
                act.activation(xn_h[:], p_a[1][:], ACT.Copy).then_inc(xn_high, 1)
                act.activation(xn[:], p_a[1][:], ACT.Copy).then_inc(xn_full, 1)

            def a_q(h):
                act.wait_ge(q_ready, h.n())
                if h.follows(1):
                    act.wait_ge(q_dma, h.n(1, times=16 * 2 * QUADS))
                act.activation(q_h[:], p_a[0][:], ACT.Identity, bias=qkv_b[:, 0:1]).then_inc(q_high, 1)

            def a_k(h):
                act.wait_ge(k_ready, h.n())
                if h.follows(1):
                    act.wait_ge(kd_ready, h.n(1))
                act.activation(k_h[:], p_a[1][:], ACT.Identity, bias=qkv_b[:, 1:2]).then_inc(k_high, 1)

            def a_v(h):
                act.wait_ge(v_ready, h.n())
                if h.follows(1):
                    act.wait_ge(v_dma, h.n(1, times=16 * 4))
                act.activation(v_tok[:], p_a[0][:], ACT.Copy).then_inc(v_kept, 1)

            def b_exp(h, p):
                act.wait_ge(scoreT_ready[p], h.n())
                if p < 2:
                    if h.follows(1):
                        act.wait_ge(attn_ready[p + 2], h.n(1))
                else:
                    act.wait_ge(attn_ready[p - 2], h.n())
                act.activation(probs[:, p % 2], p_scoreT[:].rearrange("row (win j q) -> row win j q", win=2, j=QUADS),
                               ACT.Exp, scale=SCORE_SCALE).then_inc(probs_ready[p], 1)

            def c_o(h):
                act.wait_ge(oT_ready, h.n())
                if h.follows(1):
                    act.wait_ge(proj_ready, h.n(1))
                act.activation(o_h[:], p_c[0][:], ACT.Copy).then_inc(o_high, 1)

            def c_yn(h):
                act.wait_ge(ynT_ready, h.n())
                if h.follows(1):
                    act.wait_ge(fc1_ready[1], h.n(1))
                act.activation(yn_h[:], p_c[1][:], ACT.Copy).then_inc(yn_high, 1)

            def c_silu(h, t):
                act.wait_ge(fc1_ready[t], h.n())
                if h.follows(1):
                    act.wait_ge(fc2_ready, h.n(1))
                if h.follows(1):
                    act.wait_ge(hid_low[t], h.n(1))
                act.activation(hid_h[:, t], p_c[t][:], ACT.Silu, bias=fc1_b2[:, t:t + 1]).then_inc(hid_high[t], 1)
                act.activation(hid[:, t], p_c[t][:], ACT.Silu, bias=fc1_b2[:, t:t + 1]).then_inc(hid_full[t], 1)

            def d_out(loop, c, half):
                act.wait_ge(fin_ready[half], loop.image(c))
                if loop.follows(c - 1):
                    act.wait_ge(out_dma[half], loop.image(c - 1, times=16))
                src = p_d[:].rearrange("p (v win row c) -> p v win row c", v=2, win=4, row=WIN)
                dst = out_sb[:, half, :].rearrange("p (v row win c) -> p v win row c", v=2, row=WIN, win=4)
                act.activation(dst[:, 0], src[:, 0], ACT.Identity, bias=d_col[:, 0:1])
                act.activation(dst[:, 1], src[:, 1], ACT.Identity, bias=d_col[:, 0:1]).then_inc(fin_kept[half], 1)

            def prologue(loop):
                a = loop.half(0)
                act.wait_ge(bias_kept, 1)
                a_xn(a)
                a_q(a)
                a_k(a)
                a_v(a)

            def step(loop, b, with_a, with_c, with_d):
                a, c = loop.half(b.c + 1), loop.half(b.c - 1)
                if with_c:
                    c_o(c)
                b_exp(b, 0)
                if with_a:
                    a_xn(a)
                b_exp(b, 1)
                if with_a:
                    a_q(a)
                    a_k(a)
                b_exp(b, 2)
                if with_a:
                    a_v(a)
                if with_c:
                    c_yn(c)
                if with_d:
                    d_out(loop, -1, 0)
                b_exp(b, 3)
                if with_c:
                    c_silu(c, 0)
                    c_silu(c, 1)
                if with_d:
                    d_out(loop, -1, 1)

            def step_even(loop, more, c):
                step(loop, loop.half(0), True, c, False)

            def step_odd(loop, more, d):
                step(loop, loop.half(1), more, True, d)

            def epilogue(loop):
                c = loop.half(1)
                c_o(c)
                c_yn(c)
                c_silu(c, 0)
                c_silu(c, 1)
                d_out(loop, 0, 0)
                d_out(loop, 0, 1)

            images(act, prologue, step_even, step_odd, epilogue)

        @block.vector
        def _(dve):
            dve.memset(qd_h[:].bitcast(F32), 0.0).then_inc(const_set, 1)
            dve.memset(qd_l[:].bitcast(F32), 0.0).then_inc(const_set, 1)
            dve.memset(vd[:], 0.0).then_inc(const_set, 1)
            dve.wait_ge(const_set, 3)
            for a in range(2):
                for s in range(2):
                    dve.memset(vd[64 * a:64 * a + 64, s, :, a, DH, :], 1.0).then_inc(const_set, 1)
            dve.wait_ge(ident_set, 2)
            heads = ident[:].rearrange("p (j a d) -> p a j d", j=QUADS, a=2)
            for a in range(2):
                dve.tensor_reduce(head_a[:, a:a + 1], heads[:, a], mybir.AxisListType.XY, ALU.add).then_inc(const_ready, 1)

            def load_weights():
                dve.wait_ge(wT_ready, 1)
                dve.tensor_copy(wT[:, 0:4, :], p_score[:])
                dve.tensor_copy(wT[:, 4:8, :], p_scoreT[:])
                dve.tensor_copy(wT[0:E, 9, :], p_attn[0:E, C:2 * C])
                dve.tensor_copy(wT[:, 8, :], p_attn[:, 0:C]).then_inc(wT_kept, 1)
                dve.wait_ge(bias_ready, 1)
                dve.tensor_tensor(fc1_b2[:], p_d[:, 3:5], col(FC1B, 2), ALU.add)
                dve.tensor_tensor(qkv_b[:], p_d[:, 0:3], col(INB, 3), ALU.add).then_inc(bias_kept, 1)
                dve.wait_ge(wT_kept, 1)
                dve.tensor_scalar(w_full[:, Q_:K_ + 1, :], wT[:, 0:2, :], col(G1), None, ALU.mult)
                dve.tensor_copy(w_full[:, O_, :], wT[:, 3, :])
                dve.tensor_scalar(w_full[:, F1_:F1_ + 2, :], wT[:, 4:6, :], col(G2), None, ALU.mult)
                dve.tensor_scalar(wv_cols[:].rearrange("p (a d j) -> p a d j", a=2, d=DH),
                                  wT[:, 2, :].rearrange("p (j a d) -> p a d j", j=QUADS, a=2), col(G1), None, ALU.mult)
                dve.tensor_copy(w_full[:, F2_:F2_ + 2, :], wT[:, 6:8, :]).then_inc(w_scaled, 1)
                dve.wait_ge(w_scaled, 1)
                dve.tensor_copy(wh[:], w_full[:]).then_inc(w_high, 1)
                dve.wait_ge(w_high, 1)
                dve.tensor_tensor(wl[:], w_full[:], wh[:].bitcast(F32), ALU.subtract).then_inc(w_ready, 1)
                dve.wait_ge(ob_ready, 1)
                dve.tensor_tensor(out_b2[:], p_d[:, 8:9], col(OUTB), ALU.add).then_inc(ob_kept, 1)

            def statistics(h, src, ready, stats, stats_set, mv, mv_set, read):
                dve.wait_ge(ready, h.n())
                for t in range(4):
                    last = dve.bn_stats(stats[:, t, :], src[:, C * t:C * t + C])
                last.then_inc(stats_set, 1)
                if h.follows(1):
                    dve.wait_ge(read, h.n(1))
                dve.wait_ge(stats_set, h.n())
                dve.sem_inc(dve_waits, 1)
                for t in range(4):
                    last = dve.bn_aggr(mv[:, t, :], stats[:, t, :])
                last.then_inc(mv_set, 1)

            def normalise(h, dst, src, mv, rstd, rstd_set, done, read):
                dve.wait_ge(rstd_set, h.n())
                if h.follows(1):
                    dve.wait_ge(read, h.n(1))
                for t in range(4):
                    last = dve.tensor_scalar(dst[:, t, :], src[:, C * t:C * t + C], mv[:, t, 0:1], rstd[:, t:t + 1],
                                             ALU.subtract, ALU.mult)
                last.then_inc(done, 1)

            def a_stats(h):
                statistics(h, p_a[0], xT_ready, stats1, ln1_stats, mv1, ln1_mv, xn_tok_set)

            def a_norm(h):
                normalise(h, xn_tok, p_a[0], mv1, rstd1, ln1_rstd, xn_tok_set, xnT_ready)

            def a_xn(h):
                dve.wait_ge(xn_full, h.n())
                if h.follows(1):
                    dve.wait_ge(k_ready, h.n(1))
                dve.tensor_tensor(xn_l[:], p_a[1][:], xn_h[:].bitcast(F32), ALU.subtract).then_inc(xn_low, 1)

            def a_q(h):
                dve.wait_ge(q_high, h.n())
                if h.follows(1):
                    dve.wait_ge(q_dma, h.n(1, times=16 * 2 * QUADS))
                dve.scalar_tensor_tensor(q_l[:], p_a[0][:], qkv_b[:, 0:1], q_h[:].bitcast(F32),
                                         ALU.add, ALU.subtract).then_inc(q_low, 1)

            def a_k(h):
                dve.wait_ge(k_high, h.n())
                if h.follows(1):
                    dve.wait_ge(kd_ready, h.n(1))
                dve.scalar_tensor_tensor(k_l[:], p_a[1][:], qkv_b[:, 1:2], k_h[:].bitcast(F32),
                                         ALU.add, ALU.subtract).then_inc(k_low, 1)

            def b_max(h, p):
                dve.wait_ge(score_ready[p], h.n())
                if p == 0:
                    if h.follows(1):
                        dve.wait_ge(max_wide_ready[PAIRS - 1], h.n(1))
                else:
                    dve.wait_ge(max_wide_ready[p - 1], h.n())
                dve.tensor_reduce(row_max[:], p_score[:].rearrange("row (h k) -> row h k", h=HEADS), AXIS_X, ALU.max
                                  ).then_inc(max_ready[p], 1)

            def b_norm(h, p):
                dve.wait_ge(attn_ready[p], h.n())
                if p == 0:
                    if h.follows(1):
                        dve.wait_ge(oT_ready, h.n(1))
                heads = p_attn[:, 0:HEADS * VB].rearrange("row (h d) -> row h d", h=HEADS)
                dve.reciprocal(inv_sum[:], heads[:, :, DH]).then_inc(inv_ready[p], 1)
                dve.wait_ge(inv_ready[p], h.n())
                dve.tensor_tensor(o_tok[:, p, :].rearrange("row (h d) -> row h d", h=HEADS), heads[:, :, 0:DH],
                                  inv_sum[:].unsqueeze(2).to_broadcast([128, HEADS, DH]), ALU.mult
                                  ).then_inc(o_tok_ready[p], 1)

            def c_o(h):
                dve.wait_ge(o_high, h.n())
                if h.follows(1):
                    dve.wait_ge(proj_ready, h.n(1))
                dve.tensor_tensor(o_l[:], p_c[0][:], o_h[:].bitcast(F32), ALU.subtract).then_inc(o_low, 1)

            def c_y1(h):
                dve.wait_ge(proj_ready, h.n())
                dve.wait_ge(x_res_set, h.n())
                dve.tensor_tensor(y1[:], p_c[1][:], x_res[:, h.par, :], ALU.add).then_inc(y1_ready, 1)

            def c_stats(h):
                statistics(h, p_c[0], yT_ready, stats2, ln2_stats, mv2, ln2_mv, yn_tok_set)

            def c_norm(h):
                normalise(h, yn_tok, p_c[0], mv2, rstd2, ln2_rstd, yn_tok_set, ynT_ready)

            def c_yn(h):
                dve.wait_ge(yn_high, h.n())
                dve.tensor_tensor(yn_l[:], p_c[1][:], yn_h[:].bitcast(F32), ALU.subtract).then_inc(yn_low, 1)

            def c_y2(h):
                dve.wait_ge(fc2_ready, h.n())
                if h.follows(1):
                    dve.wait_ge(y2_low, h.n(1))
                dve.wait_ge(y1_ready, h.n())
                dve.scalar_tensor_tensor(y2[:], p_c[0][:], col(FC2B), y1[:], ALU.add, ALU.add).then_inc(y2_ready, 1)

            def c_kv(h):
                dve.wait_ge(kv_ready, h.n())
                if h.follows(2):
                    dve.wait_ge(kvT_ready, h.of_parity(2))
                dve.tensor_tensor(kv_tok[:, h.par], p_c[1][:].rearrange("row (t e) -> row t e", t=4),
                                  kv_bias[:].unsqueeze(1).to_broadcast([128, 4, 2 * E]), ALU.add).then_inc(kv_kept, 1)

            def d_kvT(loop, c):
                dve.wait_ge(kvT_ready, loop.image(c))
                dve.tensor_scalar(kvT[:], p_d[0:E, 0:E], 1.0 / TOKENS, None, ALU.mult).then_inc(kvT_kept, 1)

            def d_bT(loop, c):
                dve.wait_ge(bT_ready, loop.image(c))
                dve.tensor_copy(bT[:], p_d[0:E, 0:C]).then_inc(bT_kept, 1)

            def d_mT(loop, c):
                dve.wait_ge(mT_ready, loop.image(c))
                if loop.follows(c - 1):
                    dve.wait_ge(fin_ready[1], loop.image(c - 1))
                if loop.follows(c - 1):
                    dve.wait_ge(fin_kept[1], loop.image(c - 1))
                dve.tensor_tensor(mT[:], p_d[:, 0:C], ident[:], ALU.add).then_inc(mT_kept, 1)
                dve.tensor_tensor(d_col[:], p_d[:, C:C + 1], col(BO), ALU.add).then_inc(d_kept, 1)
                dve.wait_ge(mT_kept, loop.image(c))
                dve.tensor_copy(m_h[:], mT[:]).then_inc(m_high, 1)
                dve.wait_ge(m_high, loop.image(c))
                dve.tensor_tensor(m_l[:], mT[:], m_h[:].bitcast(F32), ALU.subtract).then_inc(m_low, 1)

            def prologue(loop):
                a = loop.half(0)
                a_stats(a)
                load_weights()
                a_norm(a)
                a_xn(a)
                a_q(a)
                a_k(a)

            def step(loop, b, with_a, with_c, with_d):
                a, c = loop.half(b.c + 1), loop.half(b.c - 1)
                b_max(b, 0)
                if with_a:
                    a_stats(a)
                if with_c:
                    c_o(c)
                if with_d:
                    d_kvT(loop, -1)
                b_max(b, 1)
                if with_c:
                    c_y1(c)
                if with_a:
                    a_norm(a)
                if with_d:
                    d_bT(loop, -1)
                b_norm(b, 0)
                if with_a:
                    a_xn(a)
                b_max(b, 2)
                if with_c:
                    c_stats(c)
                if with_a:
                    a_q(a)
                if with_d:
                    d_mT(loop, -1)
                b_norm(b, 1)
                if with_c:
                    c_norm(c)
                if with_a:
                    a_k(a)
                b_max(b, 3)
                if with_c:
                    c_yn(c)
                b_norm(b, 2)
                b_norm(b, 3)
                if with_c:
                    c_y2(c)
                    c_kv(c)

            def step_even(loop, more, c):
                step(loop, loop.half(0), True, c, False)

            def step_odd(loop, more, d):
                step(loop, loop.half(1), more, True, d)

            def epilogue(loop):
                c = loop.half(1)
                c_o(c)
                c_y1(c)
                c_stats(c)
                c_norm(c)
                c_yn(c)
                c_y2(c)
                c_kv(c)
                d_kvT(loop, 0)
                d_bT(loop, 0)
                d_mT(loop, 0)

            images(dve, prologue, step_even, step_odd, epilogue)


_INS = ['x', 'L0_conv_ln1_g', 'L0_conv_ln1_b', 'L0_conv_in_w', 'L0_conv_in_b', 'L0_conv_out_w', 'L0_conv_out_b',
        'L0_conv_ln2_g', 'L0_conv_ln2_b', 'L0_conv_fc1_w', 'L0_conv_fc1_b', 'L0_conv_fc2_w', 'L0_conv_fc2_b',
        'L1_conv_wq', 'L1_conv_bq', 'L1_conv_wk', 'L1_conv_bk', 'L1_conv_wv', 'L1_conv_bv', 'L1_conv_wo', 'L1_conv_bo']


def kernel(**inputs):
    import numpy as np
    import concourse.bacc as bacc
    from concourse.bass_utils import run_bass_kernel_spmd

    nc = bacc.Bacc("TRN2", target_bir_lowering=False, num_devices=1)
    arrays, args = {}, []
    for name in _INS:
        a = np.ascontiguousarray(inputs[name])
        arrays[f"in_{name}"] = a
        args.append(nc.dram_tensor(f"in_{name}", a.shape, mybir.dt.from_np(a.dtype), kind="ExternalInput").ap())
    args.append(nc.dram_tensor("out", (IMAGES, C, SIDE, SIDE), F32, kind="ExternalOutput").ap())
    build(nc, *args)
    result = run_bass_kernel_spmd(nc, [arrays], core_ids=[0])
    return result.results[0]["out"]
```

```python
from contextlib import ExitStack

import concourse.bass as bass
from concourse import mybir

F32 = mybir.dt.float32
F32R = mybir.dt.float32r
BF16 = mybir.dt.bfloat16
ACT = mybir.ActivationFunctionType
ALU = mybir.AluOpType
AXIS_X = mybir.AxisListType.X

IMAGES, C, SIDE = 8, 128, 32
WIN = 8
KEYS = WIN * WIN
TOKENS = SIDE * SIDE
HALF = TOKENS // 2
WH = HALF // KEYS
PAIRS = WH // 2
HEADS, DH = 8, 16
QUADS = 4
HIDDEN = 256
E = 64
EPS = 1e-5
SCORE_SCALE = DH ** -0.5
VB = DH + 1
Q_, K_, O_, F1_, F2_ = 0, 1, 2, 3, 5


class Loop:

    def __init__(self, eng, i):
        self.eng, self.i, self.kept = eng, i, {}

    def number(self, a, b):
        if isinstance(self.i, int):
            return a * self.i + b
        if (a, b) not in self.kept:
            self.kept[a, b] = self.eng.snap(self.i * a + b)
        return self.kept[a, b]

    def half(self, c):
        return Half(self, c)

    def image(self, c, times=1):
        return self.number(times, times * (c + 1))

    def follows(self, c):
        return not isinstance(self.i, int) or self.i + c >= 0


class Half:

    def __init__(self, loop, c):
        self.loop, self.c, self.par = loop, c, c % 2

    def n(self, back=0, times=1):
        return self.loop.number(2 * times, times * (self.c - back + 1))

    def of_parity(self, back=0, times=1):
        return self.loop.number(times, times * ((self.c - back) // 2 + 1))

    def follows(self, back):
        return not isinstance(self.loop.i, int) or 2 * self.loop.i + self.c - back >= 0


def build(nc, x, ln1_g, ln1_b, in_w, in_b, out_w, out_b, ln2_g, ln2_b, fc1_w, fc1_b, fc2_w, fc2_b,
          wq, bq, wk, bk, wv, bv, wo, bo, out):
    ctx = ExitStack()
    with ctx:
        def sb(name, shape, dt=F32):
            return ctx.enter_context(nc.sbuf_tensor(name, shape, dt))

        def sem(name):
            return ctx.enter_context(nc.semaphore(name))

        def sems(name, n):
            return [sem(f"{name}{k}") for k in range(n)]

        in_w_rows = sb("in_w_rows", [128, 3, C])
        out_w_rows = sb("out_w_rows", [128, C])
        fc1_rows = sb("fc1_rows", [128, 2, C])
        fc2_rows = sb("fc2_rows", [128, HIDDEN])
        kv_rows = sb("kv_rows", [2 * E, C])
        wo_rows = sb("wo_rows", [C, E])
        wq_rows = sb("wq_rows", [E, C])
        cols = sb("cols", [128, 16])
        G1, B1, G2, B2, INB, OUTB, FC1B, FC2B, BO, BQ = 0, 1, 2, 3, 4, 7, 8, 10, 11, 12
        kv_bias = sb("kv_bias", [128, 2 * E])
        wT = sb("wT", [128, 10, C])
        w_full = sb("w_full", [128, 7, C])
        wh = sb("wh", [128, 7, C], F32R)
        wl = sb("wl", [128, 7, C], F32R)
        wv_cols = sb("wv_cols", [128, C])
        qkv_b = sb("qkv_b", [128, 3])
        fc1_b2 = sb("fc1_b2", [128, 2])
        out_b2 = sb("out_b2", [128, 1])
        head_a = sb("head_a", [128, 2])
        ident = sb("ident", [128, 128])
        neg_ident = sb("neg_ident", [128, 128], BF16)
        minus_half = sb("minus_half", [128, 4])
        table_sink = sb("table_sink", [128, 2])

        x_in = sb("x_in", [C, 2, HALF])
        x_res = sb("x_res", [C, 2, HALF])
        stats1 = sb("stats1", [128, 4, 6])
        mv1 = sb("mv1", [128, 4, 2])
        rstd1 = sb("rstd1", [128, 4])
        xn_tok = sb("xn_tok", [128, 4, C])
        xn = sb("xn", [C, HALF])
        xn_h = sb("xn_h", [C, HALF], F32R)
        xn_l = sb("xn_l", [C, HALF], F32R)
        q_h = sb("q_h", [C, HALF], F32R)
        q_l = sb("q_l", [C, HALF], F32R)
        k_h = sb("k_h", [C, HALF], F32R)
        k_l = sb("k_l", [C, HALF], F32R)
        v_tok = sb("v_tok", [128, PAIRS, C])
        qd_h = sb("qd_h", [C, 2, QUADS, HALF], F32R)
        qd_l = sb("qd_l", [C, 2, QUADS, HALF], F32R)
        kd_h = sb("kd_h", [C, 2, WH, 2, KEYS], F32R)
        kd_l = sb("kd_l", [C, 2, WH, 2, KEYS], F32R)
        vd = sb("vd", [128, 2, WH, 2, VB, QUADS])

        row_max = sb("row_max", [128, 2, HEADS])
        max_wide = sb("max_wide", [128, 2, HEADS, KEYS], BF16)
        probs = sb("probs", [128, 2, 2, QUADS, KEYS])
        inv_sum = sb("inv_sum", [128, HEADS])
        o_tok = sb("o_tok", [128, PAIRS, C])

        o_h = sb("o_h", [C, HALF], F32R)
        o_l = sb("o_l", [C, HALF], F32R)
        y1 = sb("y1", [C, HALF])
        stats2 = sb("stats2", [128, 4, 6])
        mv2 = sb("mv2", [128, 4, 2])
        rstd2 = sb("rstd2", [128, 4])
        yn_tok = sb("yn_tok", [128, 4, C])
        yn_h = sb("yn_h", [C, HALF], F32R)
        yn_l = sb("yn_l", [C, HALF], F32R)
        hid = sb("hid", [128, 2, HALF])
        hid_h = sb("hid_h", [128, 2, HALF], F32R)
        hid_l = sb("hid_l", [128, 2, HALF], F32R)
        y2 = sb("y2", [C, HALF])
        y2_h = sb("y2_h", [C, 2, HALF], F32R)
        y2_l = sb("y2_l", [C, 2, HALF], F32R)
        kv_tok = sb("kv_tok", [128, 2, 4, 2 * E])

        kvT = sb("kvT", [E, E])
        bT = sb("bT", [E, C])
        mT = sb("mT", [C, C])
        m_h = sb("m_h", [C, C], F32R)
        m_l = sb("m_l", [C, C], F32R)
        d_col = sb("d_col", [C, 1])
        out_sb = sb("out_sb", [C, 2, HALF])

        def bank(name, dt=F32):
            return ctx.enter_context(nc.psum_tensor(name, [128, 512], dt))

        p_score = bank("p_score")
        p_scoreT = bank("p_scoreT")
        p_attn = bank("p_attn")
        p_a = [bank("p_a0"), bank("p_a1")]
        p_c = [bank("p_c0"), bank("p_c1")]
        p_d = bank("p_d")

        w_dma = sem("w_dma")
        const_set, ident_set, const_ready = sem("const_set"), sem("ident_set"), sem("const_ready")
        wT_ready, wT_kept, bias_ready, bias_kept = sem("wT_ready"), sem("wT_kept"), sem("bias_ready"), sem("bias_kept")
        ob_ready, ob_kept, w_scaled, w_high, w_ready = (
            sem("ob_ready"), sem("ob_kept"), sem("w_scaled"), sem("w_high"), sem("w_ready"))
        x_dma = sems("x_dma", 2)
        x_res_set = sem("x_res_set")
        xT_ready, ln1_stats, ln1_mv, ln1_var, ln1_rstd, xn_tok_set = (
            sem("xT_ready"), sem("ln1_stats"), sem("ln1_mv"), sem("ln1_var"), sem("ln1_rstd"), sem("xn_tok_set"))
        xnT_ready, xn_high, xn_low, xn_full = sem("xnT_ready"), sem("xn_high"), sem("xn_low"), sem("xn_full")
        q_ready, q_high, q_low, k_ready, k_high, k_low = (
            sem("q_ready"), sem("q_high"), sem("q_low"), sem("k_ready"), sem("k_high"), sem("k_low"))
        v_ready, v_kept = sem("v_ready"), sem("v_kept")
        q_high_dma, q_low_dma, v_dma = sem("q_high_dma"), sem("q_low_dma"), sem("v_dma")
        kd_high, kd_ready = sem("kd_high"), sem("kd_ready")
        score_ready, max_ready, max_wide_ready = sems("score_ready", 4), sems("max_ready", 4), sems("max_wide_ready", 4)
        scoreT_ready, probs_ready = sems("scoreT_ready", 4), sems("probs_ready", 4)
        attn_ready, inv_ready, o_tok_ready = sems("attn_ready", 4), sems("inv_ready", 4), sems("o_tok_ready", 4)
        oT_ready, o_high, o_low, proj_ready, y1_ready = (
            sem("oT_ready"), sem("o_high"), sem("o_low"), sem("proj_ready"), sem("y1_ready"))
        yT_ready, ln2_stats, ln2_mv, ln2_var, ln2_rstd, yn_tok_set = (
            sem("yT_ready"), sem("ln2_stats"), sem("ln2_mv"), sem("ln2_var"), sem("ln2_rstd"), sem("yn_tok_set"))
        ynT_ready, yn_high, yn_low = sem("ynT_ready"), sem("yn_high"), sem("yn_low")
        fc1_ready, hid_high, hid_full, hid_low = sems("fc1_ready", 2), sems("hid_high", 2), sems("hid_full", 2), sems("hid_low", 2)
        fc2_ready, y2_ready, y2_high, y2_low = sem("fc2_ready"), sem("y2_ready"), sem("y2_high"), sem("y2_low")
        kv_ready, kv_kept = sem("kv_ready"), sem("kv_kept")
        kvT_ready, kvT_kept, bT_ready, bT_kept = sem("kvT_ready"), sem("kvT_kept"), sem("bT_ready"), sem("bT_kept")
        mT_ready, mT_kept, m_high, m_low, d_kept = sem("mT_ready"), sem("mT_kept"), sem("m_high"), sem("m_low"), sem("d_kept")
        fin_ready, fin_kept = sems("fin_ready", 2), sems("fin_kept", 2)
        out_dma = sems("out_dma", 2)
        exp_table, silu_table = sem("exp_table"), sem("silu_table")
        pool_waits, pe_waits, dve_waits = sem("pool_waits"), sem("pe_waits"), sem("dve_waits")

        W_LOADS = 20

        def col(k, n=1, rows=128):
            return cols[0:rows, k:k + n]

        def in_windows(half, v):
            return half.rearrange("p (v win row c) -> p v win row c", v=2, win=4, row=WIN)[:, v]

        def in_rows(half, v):
            return half.rearrange("p (v row win c) -> p v win row c", v=2, row=WIN, win=4)[:, v]

        def images(eng, prologue, step_even, step_odd, epilogue):
            prologue(Loop(eng, 0))
            first, last = Loop(eng, 0), Loop(eng, IMAGES - 1)
            step_even(first, more=True, c=False)
            step_odd(first, more=True, d=False)
            with eng.Fori(1, IMAGES - 1) as i:
                body = Loop(eng, i)
                step_even(body, more=True, c=True)
                step_odd(body, more=True, d=True)
            step_even(last, more=False, c=True)
            step_odd(last, more=False, d=True)
            epilogue(last)

        block = ctx.enter_context(nc.Block())

        @block.sync
        def _(sp):
            def load(dst, src):
                sp.dma_start(dst, src).then_inc(w_dma, 16)

            def column(v, n=1):
                return v.rearrange("(n p) -> p n", n=n)

            x_rows = x.rearrange("b c (h row) win -> b h c (row win)", h=2)

            def load_x(h):
                src = x_rows[h.loop.number(1, h.c // 2), h.par]
                if h.follows(2):
                    sp.wait_ge(xT_ready, h.n(2))
                if h.follows(2):
                    sp.wait_ge(x_res_set, h.n(2))
                sp.dma_start(x_in[:, h.par, :], src).then_inc(x_dma[h.par], 16)

            first = Loop(sp, 0)
            load_x(first.half(0))
            load(in_w_rows[:], in_w.rearrange("(n p) c -> p n c", n=3))
            load(out_w_rows[:], out_w)
            load(fc1_rows[:], fc1_w.rearrange("(n p) c -> p n c", n=2))
            load(fc2_rows[:], fc2_w)
            load(kv_rows[0:E, :], wk)
            load(kv_rows[E:2 * E, :], wv)
            load(wo_rows[:], wo)
            load(wq_rows[:], wq)
            with nc.allow_non_contiguous_dma(reason="biases and gains, one element per partition"):
                load(col(INB, 3), column(in_b, 3))
                load(col(FC1B, 2), column(fc1_b, 2))
                for k, v in ((G1, ln1_g), (B1, ln1_b), (G2, ln2_g), (B2, ln2_b), (OUTB, out_b),
                             (FC2B, fc2_b), (BO, bo)):
                    load(col(k), column(v))
                load(col(BQ, rows=E), column(bq))
            load(kv_bias[:, 0:E], bass.AP(bk.tensor, 0, [[0, 128], [1, E]]))
            load(kv_bias[:, E:2 * E], bass.AP(bv.tensor, 0, [[0, 128], [1, E]]))

            def spread_q(h):
                sp.wait_ge(q_high, h.n())
                if h.follows(2):
                    sp.wait_ge(scoreT_ready[PAIRS - 1], h.n(2))
                for j in range(QUADS):
                    head_pair = slice(32 * j, 32 * j + 32)
                    sp.dma_start(qd_h[head_pair, h.par, j, :].bitcast(F32), q_h[head_pair, :].bitcast(F32)).then_inc(q_high_dma, 16)
                sp.wait_ge(q_low, h.n())
                for j in range(QUADS):
                    head_pair = slice(32 * j, 32 * j + 32)
                    sp.dma_start(qd_l[head_pair, h.par, j, :].bitcast(F32), q_l[head_pair, :].bitcast(F32)).then_inc(q_low_dma, 16)

            def spread_v(h):
                sp.wait_ge(v_kept, h.n())
                if h.follows(2):
                    sp.wait_ge(attn_ready[PAIRS - 1], h.n(2))
                slot = vd[:, h.par].rearrange("row (p win) a d j -> row p win a (d j)", win=2)
                for a in range(2):
                    for win in range(2):
                        sp.dma_start(slot[64 * a:64 * a + 64, :, win, a, 0:KEYS],
                                     v_tok[64 * win:64 * win + 64, :, 64 * a:64 * a + 64]).then_inc(v_dma, 16)

            def store(loop, c):
                for half in range(2):
                    dst = out.rearrange("b c (h row) win -> b h c (row win)", h=2)[loop.number(1, c), half]
                    sp.wait_ge(fin_kept[half], loop.image(c))
                    sp.dma_start(dst, out_sb[:, half, :]).then_inc(out_dma[half], 16)

            def prologue(loop):
                sp.wait_ge(const_set, 7)
                spread_q(loop.half(0))
                spread_v(loop.half(0))
                load_x(loop.half(1))

            def step_even(loop, more, c):
                if more:
                    load_x(loop.half(2))
                spread_q(loop.half(1))
                spread_v(loop.half(1))

            def step_odd(loop, more, d):
                if more:
                    load_x(loop.half(3))
                    spread_q(loop.half(2))
                    spread_v(loop.half(2))
                if d:
                    store(loop, -1)

            def epilogue(loop):
                store(loop, 0)
                for half in range(2):
                    sp.wait_ge(out_dma[half], 16 * IMAGES)

            images(sp, prologue, step_even, step_odd, epilogue)


        @block.gpsimd
        def _(pool):
            pool.memset(ident[:], 0.0).then_inc(ident_set, 1)
            pool.wait_ge(ident_set, 1)
            pool.affine_select(out=ident[:], in_=ident[:], compare_op=ALU.not_equal, fill=1.0, base=0,
                               pattern=[[-1, 128]], channel_multiplier=1).then_inc(ident_set, 1)
            pool.wait_ge(ident_set, 2)
            pool.tensor_scalar(neg_ident[:], ident[:], -1.0, None, ALU.mult).then_inc(const_ready, 1)
            pool.memset(minus_half[:], -0.5).then_inc(const_ready, 1)

            def waited():
                pool.sem_inc(pool_waits, 1)

            def residual(h):
                pool.wait_ge(x_dma[h.par], h.of_parity(times=16))
                if h.follows(2):
                    pool.wait_ge(y1_ready, h.n(2))
                waited()
                for v in range(2):
                    last = pool.tensor_scalar(in_windows(x_res[:, h.par, :], v), in_rows(x_in[:, h.par, :], v),
                                              out_b2[:, 0:1], None, ALU.add)
                last.then_inc(x_res_set, 1)

            def rstd(h, mv, mv_set, var_set, out_, out_set, read):
                pool.wait_ge(mv_set, h.n())
                if h.follows(1):
                    pool.wait_ge(read, h.n(1))
                waited()
                pool.tensor_scalar(out_[:], mv[:, :, 1], EPS, None, ALU.add).then_inc(var_set, 1)
                pool.wait_ge(var_set, h.n())
                pool.tensor_tensor(out_[:], out_[:], minus_half[:], ALU.pow).then_inc(out_set, 1)

            def hidden_low(h, t):
                pool.wait_ge(hid_high[t], h.n())
                pool.wait_ge(hid_full[t], h.n())
                if h.follows(1):
                    pool.wait_ge(fc2_ready, h.n(1))
                pool.tensor_tensor(hid_l[:, t], hid[:, t], hid_h[:, t].bitcast(F32), ALU.subtract).then_inc(hid_low[t], 1)

            def y2_low_part(h):
                pool.wait_ge(y2_high, h.n())
                pool.tensor_tensor(y2_l[:, h.par], y2[:], y2_h[:, h.par].bitcast(F32), ALU.subtract).then_inc(y2_low, 1)

            def rstd1_of(h):
                rstd(h, mv1, ln1_mv, ln1_var, rstd1, ln1_rstd, xn_tok_set)

            def rstd2_of(h):
                rstd(h, mv2, ln2_mv, ln2_var, rstd2, ln2_rstd, yn_tok_set)

            def prologue(loop):
                rstd1_of(loop.half(0))
                pool.wait_ge(ob_kept, 1)
                residual(loop.half(0))
                rstd1_of(loop.half(1))

            def step(loop, b, with_a, with_next, with_c, with_tail):
                a, next_a, c, tail = loop.half(b.c + 1), loop.half(b.c + 2), loop.half(b.c - 1), loop.half(b.c - 2)
                if with_tail:
                    y2_low_part(tail)
                if with_a:
                    residual(a)
                if with_c:
                    rstd2_of(c)
                if with_next:
                    rstd1_of(next_a)
                if with_c:
                    hidden_low(c, 0)
                    hidden_low(c, 1)

            def step_even(loop, more, c):
                step(loop, loop.half(0), True, more, c, c)

            def step_odd(loop, more, d):
                step(loop, loop.half(1), more, more, True, d)

            def epilogue(loop):
                c = loop.half(1)
                y2_low_part(loop.half(0))
                rstd2_of(c)
                hidden_low(c, 0)
                hidden_low(c, 1)
                y2_low_part(c)

            images(pool, prologue, step_even, step_odd, epilogue)

        @block.tensor
        def _(pe):
            def three_passes(dst, blocks, moving):
                passes = [(weight, moving_part) for (b_h, b_l), (m_h, m_l) in zip(blocks, moving)
                          for weight, moving_part in ((b_h, m_h), (b_h, m_l), (b_l, m_h))]
                for k, (weight, moving_part) in enumerate(passes):
                    last = pe.matmul(dst, weight, moving_part, start=k == 0, stop=k == len(passes) - 1)
                return last

            def weights(b):
                return wh[:, b, :], wl[:, b, :]

            def load_weights():
                pe.wait_ge(w_dma, 16 * W_LOADS)
                pe.wait_ge(ident_set, 2)
                blocks = [in_w_rows[:, k, :] for k in range(3)] + [out_w_rows[:]] + \
                         [fc1_rows[:, k, :] for k in range(2)] + [fc2_rows[:, 0:C], fc2_rows[:, C:2 * C]] + [kv_rows[:]]
                banks = [p_score, p_scoreT, p_attn]
                for k, weight in enumerate(blocks):
                    pe.transpose(banks[k // 4][:, C * (k % 4):C * (k % 4) + C], weight, ident[:])
                pe.transpose(p_attn[0:E, C:2 * C], wo_rows[:], ident[:]).then_inc(wT_ready, 1)
                pe.wait_ge(wT_kept, 1)
                for k, (b, v) in enumerate(((0, B1), (1, B1), (2, B1), (4, B2), (5, B2))):
                    last = pe.matmul(p_d[:, k:k + 1], wT[:, b, :], col(v), start=True, stop=True)
                last.then_inc(bias_ready, 1)
                pe.wait_ge(bias_kept, 1)
                pe.matmul(p_d[:, 8:9], wT[:, 3, :], qkv_b[:, 2:3], start=True, stop=True).then_inc(ob_ready, 1)

            def a_transpose(h):
                pe.wait_ge(x_dma[h.par], h.of_parity(times=16))
                if h.follows(1):
                    pe.wait_ge(v_kept, h.n(1))
                for t in range(4):
                    last = pe.transpose(p_a[0][:, C * t:C * t + C], x_in[:, h.par, C * t:C * t + C], ident[:])
                last.then_inc(xT_ready, 1)

            def a_back(h):
                pe.wait_ge(xn_tok_set, h.n())
                if h.follows(1):
                    pe.wait_ge(k_high, h.n(1))
                if h.follows(1):
                    pe.wait_ge(k_low, h.n(1))
                for t in range(4):
                    last = pe.transpose(p_a[1][:, C * t:C * t + C], xn_tok[:, t, :], ident[:])
                last.then_inc(xnT_ready, 1)

            def a_q(h):
                pe.wait_ge(xn_high, h.n())
                pe.wait_ge(xn_low, h.n())
                three_passes(p_a[0][:], [weights(Q_)], [(xn_h[:], xn_l[:])]).then_inc(q_ready, 1)

            def a_k(h):
                pe.wait_ge(xn_full, h.n())
                three_passes(p_a[1][:], [weights(K_)], [(xn_h[:], xn_l[:])]).then_inc(k_ready, 1)

            def a_v(h):
                pe.wait_ge(q_high, h.n())
                pe.wait_ge(q_low, h.n())
                for p in range(PAIRS):
                    last = pe.matmul(p_a[0][:, C * p:C * p + C], xn[:, C * p:C * p + C], wv_cols[:],
                                     start=True, stop=True)
                last.then_inc(v_ready, 1)

            def b_score(h, p):
                if p == 0:
                    pe.wait_ge(q_high_dma, h.n(times=16 * QUADS))
                    pe.wait_ge(kd_high, h.n())
                    if h.follows(1):
                        pe.wait_ge(max_ready[PAIRS - 1], h.n(1))
                else:
                    pe.wait_ge(max_ready[p - 1], h.n())
                for j in range(QUADS):
                    for win, rows in ((1, 2 * KEYS), (0, KEYS)):
                        last = pe.matmul(p_score[0:rows, 2 * KEYS * j:2 * KEYS * (j + 1)],
                                         qd_h[:, h.par, j, 2 * KEYS * p:2 * KEYS * p + rows],
                                         kd_h[:, h.par, 2 * p + win], start=True, stop=True)
                last.then_inc(score_ready[p], 1)

            def b_scoreT(h, p):
                pe.wait_ge(max_wide_ready[p], h.n())
                if p == 0:
                    pe.wait_ge(q_low_dma, h.n(times=16 * QUADS))
                    pe.wait_ge(kd_ready, h.n())
                    if h.follows(1):
                        pe.wait_ge(probs_ready[PAIRS - 1], h.n(1))
                else:
                    pe.wait_ge(probs_ready[p - 1], h.n())
                dst = p_scoreT[:].rearrange("row (win j q) -> row win j q", win=2, j=QUADS)
                for j in range(QUADS):
                    pe.matmul(dst[:, :, j, :], max_wide[:, p % 2, 2 * j:2 * j + 2, :],
                              neg_ident[:], start=j == 0, stop=False, skip_group_check=True)
                for win in range(2):
                    window = 2 * p + win
                    for k, (kd, qd) in enumerate(((kd_h, qd_h), (kd_h, qd_l), (kd_l, qd_h))):
                        last = pe.matmul(dst[:, win], kd[:, h.par, window], qd[:, h.par, :, KEYS * window:KEYS * (window + 1)],
                                         start=False, stop=win == 1 and k == 2, skip_group_check=True)
                last.then_inc(scoreT_ready[p], 1)

            def b_attn(h, p):
                pe.wait_ge(probs_ready[p], h.n())
                if p == 0:
                    pe.wait_ge(v_dma, h.n(times=16 * 4))
                    if h.follows(1):
                        pe.wait_ge(o_tok_ready[PAIRS - 1], h.n(1))
                else:
                    pe.wait_ge(o_tok_ready[p - 1], h.n())
                for win in range(2):
                    for j in range(QUADS):
                        last = pe.matmul(p_attn[64 * win:64 * win + 64, 2 * VB * j:2 * VB * (j + 1)],
                                         probs[:, p % 2, win, j, :],
                                         vd[:, h.par, 2 * p + win, :, :, j].rearrange("row a d -> row (a d)"),
                                         start=True, stop=True)
                last.then_inc(attn_ready[p], 1)

            def c_transpose(h):
                pe.wait_ge(o_tok_ready[PAIRS - 1], h.n())
                if h.follows(1):
                    pe.wait_ge(hid_high[1], h.n(1))
                if h.follows(1):
                    pe.wait_ge(hid_full[1], h.n(1))
                for p in range(PAIRS):
                    last = pe.transpose(p_c[1][:, C * p:C * p + C], o_tok[:, p, :], ident[:])
                last.then_inc(oT_ready, 1)

            def c_project(h):
                pe.wait_ge(o_high, h.n())
                pe.wait_ge(o_low, h.n())
                three_passes(p_c[1][:], [weights(O_)], [(o_h[:], o_l[:])]).then_inc(proj_ready, 1)

            def c_yT(h):
                pe.wait_ge(y1_ready, h.n())
                if h.follows(1):
                    pe.wait_ge(kv_kept, h.n(1))
                for t in range(4):
                    last = pe.transpose(p_c[0][:, C * t:C * t + C], y1[:, C * t:C * t + C], ident[:])
                last.then_inc(yT_ready, 1)

            def c_back(h):
                pe.wait_ge(yn_tok_set, h.n())
                for t in range(4):
                    last = pe.transpose(p_c[1][:, C * t:C * t + C], yn_tok[:, t, :], ident[:])
                last.then_inc(ynT_ready, 1)

            def c_fc1(h, t):
                pe.wait_ge(yn_high, h.n())
                pe.wait_ge(yn_low, h.n())
                three_passes(p_c[t][:], [weights(F1_ + t)], [(yn_h[:], yn_l[:])]).then_inc(fc1_ready[t], 1)

            def c_fc2(h):
                pe.wait_ge(hid_high[0], h.n())
                pe.wait_ge(hid_low[0], h.n())
                pe.wait_ge(hid_high[1], h.n())
                pe.wait_ge(hid_low[1], h.n())
                three_passes(p_c[0][:], [weights(F2_), weights(F2_ + 1)],
                             [(hid_h[:, t], hid_l[:, t]) for t in range(2)]).then_inc(fc2_ready, 1)

            def c_kv(h):
                pe.wait_ge(y2_ready, h.n())
                for t in range(4):
                    last = pe.matmul(p_c[0][:, C * t:C * t + C], y2[:, C * t:C * t + C], wT[:, 8, :],
                                     start=True, stop=True)
                last.then_inc(kv_ready, 1)

            def d_kvT(loop, c):
                pe.wait_ge(kv_kept, loop.number(2, 2 * c + 2))
                if loop.follows(c - 1):
                    pe.wait_ge(fin_kept[1], loop.image(c - 1))
                for n in range(8):
                    tile = kv_tok[:, n // 4, n % 4]
                    last = pe.matmul(p_d[0:E, 0:E], tile[:, E:2 * E], tile[:, 0:E], start=n == 0, stop=n == 7)
                last.then_inc(kvT_ready, 1)

            def d_bT(loop, c):
                pe.wait_ge(kvT_kept, loop.image(c))
                pe.sem_inc(pe_waits, 1)
                pe.matmul(p_d[0:E, 0:C], kvT[:], wT[0:E, 9, :], start=True, stop=True).then_inc(bT_ready, 1)

            def d_mT(loop, c):
                pe.wait_ge(bT_kept, loop.image(c))
                pe.matmul(p_d[:, 0:C], wq_rows[:], bT[:], start=True, stop=True)
                pe.matmul(p_d[:, C:C + 1], bT[:], col(BQ, rows=E), start=True, stop=True).then_inc(mT_ready, 1)

            def d_final(loop, c, half):
                if half == 0:
                    pe.wait_ge(m_high, loop.image(c))
                    pe.wait_ge(m_low, loop.image(c))
                    pe.wait_ge(d_kept, loop.image(c))
                    pe.wait_ge(y2_low, loop.number(2, 2 * c + 2))
                else:
                    pe.wait_ge(fin_kept[0], loop.image(c))
                three_passes(p_d[:], [(m_h[:], m_l[:])], [(y2_h[:, half], y2_l[:, half])]).then_inc(fin_ready[half], 1)

            def prologue(loop):
                a = loop.half(0)
                pe.wait_ge(ident_set, 2)
                a_transpose(a)
                load_weights()
                a_back(a)
                pe.wait_ge(w_ready, 1)
                a_q(a)
                a_k(a)
                a_v(a)
                a_transpose(loop.half(1))

            def step(loop, b, with_a, with_next, with_c, with_tail, with_d):
                a, next_a, c, tail = loop.half(b.c + 1), loop.half(b.c + 2), loop.half(b.c - 1), loop.half(b.c - 2)
                b_score(b, 0)
                if with_c:
                    c_transpose(c)
                if with_a:
                    a_back(a)
                b_score(b, 1)
                if with_tail:
                    c_fc2(tail)
                b_scoreT(b, 0)
                b_score(b, 2)
                if with_tail:
                    c_kv(tail)
                if with_c:
                    c_project(c)
                b_attn(b, 0)
                if with_c:
                    c_yT(c)
                b_scoreT(b, 1)
                b_score(b, 3)
                if with_a:
                    a_q(a)
                if with_d:
                    d_kvT(loop, -1)
                b_attn(b, 1)
                if with_a:
                    a_k(a)
                    a_v(a)
                if with_d:
                    d_bT(loop, -1)
                b_scoreT(b, 2)
                if with_c:
                    c_back(c)
                if with_next:
                    a_transpose(next_a)
                if with_d:
                    d_mT(loop, -1)
                b_attn(b, 2)
                b_scoreT(b, 3)
                if with_d:
                    d_final(loop, -1, 0)
                if with_c:
                    c_fc1(c, 0)
                    c_fc1(c, 1)
                b_attn(b, 3)
                if with_d:
                    d_final(loop, -1, 1)

            def step_even(loop, more, c):
                step(loop, loop.half(0), True, more, c, c, False)

            def step_odd(loop, more, d):
                step(loop, loop.half(1), more, more, True, d, d)

            def epilogue(loop):
                c = loop.half(1)
                c_fc2(loop.half(0))
                c_transpose(c)
                c_kv(loop.half(0))
                c_project(c)
                c_yT(c)
                c_back(c)
                c_fc1(c, 0)
                c_fc1(c, 1)
                c_fc2(c)
                c_kv(c)
                d_kvT(loop, 0)
                d_bT(loop, 0)
                d_mT(loop, 0)
                d_final(loop, 0, 0)
                d_final(loop, 0, 1)

            images(pe, prologue, step_even, step_odd, epilogue)

        @block.scalar
        def _(act):
            def load_exp_table(h):
                if h.follows(1):
                    act.wait_ge(exp_table, h.n(1))
                act.activation(table_sink[:, 0:1], ident[:, 0:1], ACT.Exp).then_inc(exp_table, 1)

            def load_silu_table(h):
                if h.follows(1):
                    act.wait_ge(silu_table, h.n(1))
                act.activation(table_sink[:, 1:2], ident[:, 0:1], ACT.Silu).then_inc(silu_table, 1)

            def a_xn(h):
                act.wait_ge(xnT_ready, h.n())
                if h.follows(1):
                    act.wait_ge(q_ready, h.n(1))
                if h.follows(1):
                    act.wait_ge(v_ready, h.n(1))
                for dst, done in ((xn_h, xn_high), (xn, xn_full)):
                    for v in range(2):
                        last = act.activation(in_windows(dst[:], v), in_rows(p_a[1][:], v), ACT.Copy)
                    last.then_inc(done, 1)

            def a_q(h):
                act.wait_ge(q_ready, h.n())
                if h.follows(1):
                    act.wait_ge(q_high_dma, h.n(1, times=16 * QUADS))
                act.activation(q_h[:], p_a[0][:], ACT.Identity, bias=qkv_b[:, 0:1]).then_inc(q_high, 1)

            def a_k(h):
                act.wait_ge(k_ready, h.n())
                if h.follows(1):
                    act.wait_ge(kd_high, h.n(1))
                act.activation(k_h[:], p_a[1][:], ACT.Identity, bias=qkv_b[:, 1:2]).then_inc(k_high, 1)

            def a_v(h):
                act.wait_ge(v_ready, h.n())
                if h.follows(1):
                    act.wait_ge(v_dma, h.n(1, times=16 * 4))
                act.activation(v_tok[:], p_a[0][:], ACT.Copy).then_inc(v_kept, 1)

            def b_exp(h, p):
                act.wait_ge(scoreT_ready[p], h.n())
                if p < 2:
                    if h.follows(1):
                        act.wait_ge(attn_ready[p + 2], h.n(1))
                else:
                    act.wait_ge(attn_ready[p - 2], h.n())
                act.activation(probs[:, p % 2], p_scoreT[:].rearrange("row (win j q) -> row win j q", win=2, j=QUADS),
                               ACT.Exp, scale=SCORE_SCALE).then_inc(probs_ready[p], 1)

            def b_widen(h, p):
                act.wait_ge(max_ready[p], h.n())
                if p < 2:
                    if h.follows(1):
                        act.wait_ge(scoreT_ready[p + 2], h.n(1))
                else:
                    act.wait_ge(scoreT_ready[p - 2], h.n())
                act.activation(max_wide[:, p % 2], row_max[:, p % 2].unsqueeze(2).to_broadcast([128, HEADS, KEYS]),
                               ACT.Copy).then_inc(max_wide_ready[p], 1)

            def c_y2(h):
                act.wait_ge(y2_ready, h.n())
                if h.follows(2):
                    act.wait_ge(fin_ready[h.par], h.of_parity(2))
                act.activation(y2_h[:, h.par], y2[:], ACT.Copy).then_inc(y2_high, 1)

            def c_o(h):
                act.wait_ge(oT_ready, h.n())
                if h.follows(1):
                    act.wait_ge(proj_ready, h.n(1))
                act.activation(o_h[:], p_c[1][:], ACT.Copy).then_inc(o_high, 1)

            def c_yn(h):
                act.wait_ge(ynT_ready, h.n())
                if h.follows(1):
                    act.wait_ge(fc1_ready[1], h.n(1))
                act.activation(yn_h[:], p_c[1][:], ACT.Copy).then_inc(yn_high, 1)

            def c_silu(h, t):
                act.wait_ge(fc1_ready[t], h.n())
                if h.follows(1):
                    act.wait_ge(fc2_ready, h.n(1))
                if h.follows(1):
                    act.wait_ge(hid_low[t], h.n(1))
                act.activation(hid_h[:, t], p_c[t][:], ACT.Silu, bias=fc1_b2[:, t:t + 1]).then_inc(hid_high[t], 1)
                act.activation(hid[:, t], p_c[t][:], ACT.Silu, bias=fc1_b2[:, t:t + 1]).then_inc(hid_full[t], 1)

            def d_out(loop, c, half):
                act.wait_ge(fin_ready[half], loop.image(c))
                if loop.follows(c - 1):
                    act.wait_ge(out_dma[half], loop.image(c - 1, times=16))
                for v in range(2):
                    last = act.activation(in_rows(out_sb[:, half, :], v), in_windows(p_d[:], v), ACT.Identity,
                                          bias=d_col[:, 0:1])
                last.then_inc(fin_kept[half], 1)

            def prologue(loop):
                a = loop.half(0)
                act.wait_ge(ident_set, 2)
                act.wait_ge(bias_kept, 1)
                a_xn(a)
                a_q(a)
                a_k(a)
                a_v(a)

            def step(loop, b, with_a, with_next, with_c, with_tail, with_d):
                a, next_a, c, tail = loop.half(b.c + 1), loop.half(b.c + 2), loop.half(b.c - 1), loop.half(b.c - 2)
                if with_c:
                    c_o(c)
                if with_a:
                    a_xn(a)
                load_exp_table(b)
                b_widen(b, 1)
                b_exp(b, 0)
                if with_tail:
                    c_y2(tail)
                b_widen(b, 2)
                b_exp(b, 1)
                if with_a:
                    a_q(a)
                b_widen(b, 3)
                if with_a:
                    a_k(a)
                    a_v(a)
                b_exp(b, 2)
                if with_c:
                    c_yn(c)
                b_exp(b, 3)
                load_silu_table(b)
                if with_d:
                    d_out(loop, -1, 0)
                if with_c:
                    c_silu(c, 0)
                    c_silu(c, 1)
                if with_d:
                    d_out(loop, -1, 1)

            def step_even(loop, more, c):
                step(loop, loop.half(0), True, more, c, c, False)

            def step_odd(loop, more, d):
                step(loop, loop.half(1), more, more, True, d, d)

            def epilogue(loop):
                c = loop.half(1)
                c_y2(loop.half(0))
                c_o(c)
                c_yn(c)
                c_silu(c, 0)
                c_silu(c, 1)
                c_y2(c)
                d_out(loop, 0, 0)
                d_out(loop, 0, 1)

            images(act, prologue, step_even, step_odd, epilogue)

        @block.vector
        def _(dve):
            dve.memset(qd_h[:].bitcast(F32), 0.0).then_inc(const_set, 1)
            dve.memset(qd_l[:].bitcast(F32), 0.0).then_inc(const_set, 1)
            dve.memset(vd[:], 0.0).then_inc(const_set, 1)
            dve.wait_ge(const_set, 3)
            for a in range(2):
                for s in range(2):
                    dve.memset(vd[64 * a:64 * a + 64, s, :, a, DH, :], 1.0).then_inc(const_set, 1)
            dve.wait_ge(ident_set, 2)
            heads = ident[:].rearrange("p (j a d) -> p a j d", j=QUADS, a=2)
            for a in range(2):
                dve.tensor_reduce(head_a[:, a:a + 1], heads[:, a], mybir.AxisListType.XY, ALU.add).then_inc(const_ready, 1)

            def load_weights():
                dve.wait_ge(wT_ready, 1)
                dve.tensor_copy(wT[:, 0:4, :], p_score[:])
                dve.tensor_copy(wT[:, 4:8, :], p_scoreT[:])
                dve.tensor_copy(wT[0:E, 9, :], p_attn[0:E, C:2 * C])
                dve.tensor_copy(wT[:, 8, :], p_attn[:, 0:C]).then_inc(wT_kept, 1)
                dve.wait_ge(bias_ready, 1)
                dve.tensor_tensor(fc1_b2[:], p_d[:, 3:5], col(FC1B, 2), ALU.add)
                dve.tensor_tensor(qkv_b[:], p_d[:, 0:3], col(INB, 3), ALU.add).then_inc(bias_kept, 1)
                dve.wait_ge(wT_kept, 1)
                dve.tensor_scalar(w_full[:, Q_:K_ + 1, :], wT[:, 0:2, :], col(G1), None, ALU.mult)
                dve.tensor_copy(w_full[:, O_, :], wT[:, 3, :])
                dve.tensor_scalar(w_full[:, F1_:F1_ + 2, :], wT[:, 4:6, :], col(G2), None, ALU.mult)
                dve.tensor_scalar(wv_cols[:].rearrange("p (a d j) -> p a d j", a=2, d=DH),
                                  wT[:, 2, :].rearrange("p (j a d) -> p a d j", j=QUADS, a=2), col(G1), None, ALU.mult)
                dve.tensor_copy(w_full[:, F2_:F2_ + 2, :], wT[:, 6:8, :]).then_inc(w_scaled, 1)
                dve.wait_ge(w_scaled, 1)
                dve.tensor_copy(wh[:], w_full[:]).then_inc(w_high, 1)
                dve.wait_ge(w_high, 1)
                dve.tensor_tensor(wl[:], w_full[:], wh[:].bitcast(F32), ALU.subtract).then_inc(w_ready, 1)
                dve.wait_ge(ob_ready, 1)
                dve.tensor_tensor(out_b2[:], p_d[:, 8:9], col(OUTB), ALU.add).then_inc(ob_kept, 1)

            def statistics(h, src, ready, stats, stats_set, mv, mv_set, read):
                dve.wait_ge(ready, h.n())
                for t in range(4):
                    last = dve.bn_stats(stats[:, t, :], src[:, C * t:C * t + C])
                last.then_inc(stats_set, 1)
                if h.follows(1):
                    dve.wait_ge(read, h.n(1))
                dve.wait_ge(stats_set, h.n())
                dve.sem_inc(dve_waits, 1)
                for t in range(4):
                    last = dve.bn_aggr(mv[:, t, :], stats[:, t, :])
                last.then_inc(mv_set, 1)

            def normalise(h, dst, src, mv, rstd, rstd_set, done, read):
                dve.wait_ge(rstd_set, h.n())
                if h.follows(1):
                    dve.wait_ge(read, h.n(1))
                for t in range(4):
                    last = dve.tensor_scalar(dst[:, t, :], src[:, C * t:C * t + C], mv[:, t, 0:1], rstd[:, t:t + 1],
                                             ALU.subtract, ALU.mult)
                last.then_inc(done, 1)

            def a_stats(h):
                statistics(h, p_a[0], xT_ready, stats1, ln1_stats, mv1, ln1_mv, xn_tok_set)

            def a_norm(h):
                normalise(h, xn_tok, p_a[0], mv1, rstd1, ln1_rstd, xn_tok_set, xnT_ready)

            def a_xn(h):
                dve.wait_ge(xn_full, h.n())
                if h.follows(1):
                    dve.wait_ge(k_ready, h.n(1))
                for v in range(2):
                    last = dve.tensor_tensor(in_windows(xn_l[:], v), in_rows(p_a[1][:], v),
                                             in_windows(xn_h[:].bitcast(F32), v), ALU.subtract)
                last.then_inc(xn_low, 1)

            def a_q(h):
                dve.wait_ge(q_high, h.n())
                if h.follows(1):
                    dve.wait_ge(q_low_dma, h.n(1, times=16 * QUADS))
                dve.scalar_tensor_tensor(q_l[:], p_a[0][:], qkv_b[:, 0:1], q_h[:].bitcast(F32),
                                         ALU.add, ALU.subtract).then_inc(q_low, 1)

            def a_k(h):
                dve.wait_ge(k_high, h.n())
                if h.follows(1):
                    dve.wait_ge(kd_ready, h.n(1))
                dve.scalar_tensor_tensor(k_l[:], p_a[1][:], qkv_b[:, 1:2], k_h[:].bitcast(F32),
                                         ALU.add, ALU.subtract).then_inc(k_low, 1)

            def spread_k(h, src, dst, done):
                if h.follows(2):
                    dve.wait_ge(scoreT_ready[PAIRS - 1], h.n(2))
                for a in range(2):
                    last = dve.tensor_scalar(dst[:, h.par, :, a, :],
                                             src[:].bitcast(F32).rearrange("p (win k) -> p win k", k=KEYS),
                                             head_a[:, a:a + 1], None, ALU.mult)
                last.then_inc(done, 1)

            def a_k_blocks(h):
                dve.wait_ge(k_high, h.n())
                spread_k(h, k_h, kd_h, kd_high)

            def a_k_low_blocks(h):
                dve.wait_ge(k_low, h.n())
                spread_k(h, k_l, kd_l, kd_ready)

            def b_max(h, p):
                dve.wait_ge(score_ready[p], h.n())
                if p < 2:
                    if h.follows(1):
                        dve.wait_ge(max_wide_ready[p + 2], h.n(1))
                else:
                    dve.wait_ge(max_wide_ready[p - 2], h.n())
                dve.tensor_reduce(row_max[:, p % 2], p_score[:].rearrange("row (h k) -> row h k", h=HEADS), AXIS_X, ALU.max
                                  ).then_inc(max_ready[p], 1)

            def b_widen_first(h):
                dve.wait_ge(max_ready[0], h.n())
                if h.follows(1):
                    dve.wait_ge(scoreT_ready[2], h.n(1))
                dve.tensor_copy(max_wide[:, 0], row_max[:, 0].unsqueeze(2).to_broadcast([128, HEADS, KEYS])
                                ).then_inc(max_wide_ready[0], 1)

            def b_norm(h, p):
                dve.wait_ge(attn_ready[p], h.n())
                if p == 0:
                    if h.follows(1):
                        dve.wait_ge(oT_ready, h.n(1))
                heads = p_attn[:, 0:HEADS * VB].rearrange("row (h d) -> row h d", h=HEADS)
                dve.reciprocal(inv_sum[:], heads[:, :, DH]).then_inc(inv_ready[p], 1)
                dve.wait_ge(inv_ready[p], h.n())
                dve.tensor_tensor(o_tok[:, p, :].rearrange("row (h d) -> row h d", h=HEADS), heads[:, :, 0:DH],
                                  inv_sum[:].unsqueeze(2).to_broadcast([128, HEADS, DH]), ALU.mult
                                  ).then_inc(o_tok_ready[p], 1)

            def c_o(h):
                dve.wait_ge(o_high, h.n())
                if h.follows(1):
                    dve.wait_ge(proj_ready, h.n(1))
                dve.tensor_tensor(o_l[:], p_c[1][:], o_h[:].bitcast(F32), ALU.subtract).then_inc(o_low, 1)

            def c_y1(h):
                dve.wait_ge(proj_ready, h.n())
                dve.wait_ge(x_res_set, h.n())
                if h.follows(1):
                    dve.wait_ge(y2_ready, h.n(1))
                dve.tensor_tensor(y1[:], p_c[1][:], x_res[:, h.par, :], ALU.add).then_inc(y1_ready, 1)

            def c_stats(h):
                statistics(h, p_c[0], yT_ready, stats2, ln2_stats, mv2, ln2_mv, yn_tok_set)

            def c_norm(h):
                normalise(h, yn_tok, p_c[0], mv2, rstd2, ln2_rstd, yn_tok_set, ynT_ready)

            def c_yn(h):
                dve.wait_ge(yn_high, h.n())
                dve.tensor_tensor(yn_l[:], p_c[1][:], yn_h[:].bitcast(F32), ALU.subtract).then_inc(yn_low, 1)

            def c_y2(h):
                dve.wait_ge(fc2_ready, h.n())
                if h.follows(1):
                    dve.wait_ge(y2_low, h.n(1))
                dve.wait_ge(y1_ready, h.n())
                dve.scalar_tensor_tensor(y2[:], p_c[0][:], col(FC2B), y1[:], ALU.add, ALU.add).then_inc(y2_ready, 1)

            def c_kv(h):
                dve.wait_ge(kv_ready, h.n())
                if h.follows(2):
                    dve.wait_ge(kvT_ready, h.of_parity(2))
                dve.tensor_tensor(kv_tok[:, h.par], p_c[0][:].rearrange("row (t e) -> row t e", t=4),
                                  kv_bias[:].unsqueeze(1).to_broadcast([128, 4, 2 * E]), ALU.add).then_inc(kv_kept, 1)

            def d_kvT(loop, c):
                dve.wait_ge(kvT_ready, loop.image(c))
                dve.tensor_scalar(kvT[:], p_d[0:E, 0:E], 1.0 / TOKENS, None, ALU.mult).then_inc(kvT_kept, 1)

            def d_bT(loop, c):
                dve.wait_ge(bT_ready, loop.image(c))
                dve.tensor_copy(bT[:], p_d[0:E, 0:C]).then_inc(bT_kept, 1)

            def d_mT(loop, c):
                dve.wait_ge(mT_ready, loop.image(c))
                if loop.follows(c - 1):
                    dve.wait_ge(fin_ready[1], loop.image(c - 1))
                if loop.follows(c - 1):
                    dve.wait_ge(fin_kept[1], loop.image(c - 1))
                dve.tensor_tensor(mT[:], p_d[:, 0:C], ident[:], ALU.add).then_inc(mT_kept, 1)
                dve.tensor_tensor(d_col[:], p_d[:, C:C + 1], col(BO), ALU.add).then_inc(d_kept, 1)
                dve.wait_ge(mT_kept, loop.image(c))
                dve.tensor_copy(m_h[:], mT[:]).then_inc(m_high, 1)
                dve.wait_ge(m_high, loop.image(c))
                dve.tensor_tensor(m_l[:], mT[:], m_h[:].bitcast(F32), ALU.subtract).then_inc(m_low, 1)

            def prologue(loop):
                a = loop.half(0)
                a_stats(a)
                load_weights()
                a_norm(a)
                a_xn(a)
                a_q(a)
                a_k_blocks(a)
                a_k(a)
                a_k_low_blocks(a)
                a_stats(loop.half(1))
                a_norm(loop.half(1))

            def step(loop, b, with_a, with_next, with_c, with_tail, with_d):
                a, next_a, c, tail = loop.half(b.c + 1), loop.half(b.c + 2), loop.half(b.c - 1), loop.half(b.c - 2)
                b_max(b, 0)
                b_widen_first(b)
                if with_c:
                    c_o(c)
                if with_a:
                    a_xn(a)
                b_max(b, 1)
                if with_tail:
                    c_y2(tail)
                b_max(b, 2)
                if with_tail:
                    c_kv(tail)
                if with_c:
                    c_y1(c)
                b_norm(b, 0)
                if with_c:
                    c_stats(c)
                b_max(b, 3)
                if with_a:
                    a_q(a)
                if with_d:
                    d_kvT(loop, -1)
                b_norm(b, 1)
                if with_c:
                    c_norm(c)
                if with_d:
                    d_bT(loop, -1)
                if with_a:
                    a_k_blocks(a)
                    a_k(a)
                if with_c:
                    c_yn(c)
                b_norm(b, 2)
                if with_d:
                    d_mT(loop, -1)
                if with_next:
                    a_stats(next_a)
                if with_a:
                    a_k_low_blocks(a)
                if with_next:
                    a_norm(next_a)
                b_norm(b, 3)

            def step_even(loop, more, c):
                step(loop, loop.half(0), True, more, c, c, False)

            def step_odd(loop, more, d):
                step(loop, loop.half(1), more, more, True, d, d)

            def epilogue(loop):
                c = loop.half(1)
                c_y2(loop.half(0))
                c_o(c)
                c_kv(loop.half(0))
                c_y1(c)
                c_stats(c)
                c_norm(c)
                c_yn(c)
                c_y2(c)
                c_kv(c)
                d_kvT(loop, 0)
                d_bT(loop, 0)
                d_mT(loop, 0)

            images(dve, prologue, step_even, step_odd, epilogue)


_INS = ['x', 'L0_conv_ln1_g', 'L0_conv_ln1_b', 'L0_conv_in_w', 'L0_conv_in_b', 'L0_conv_out_w', 'L0_conv_out_b',
        'L0_conv_ln2_g', 'L0_conv_ln2_b', 'L0_conv_fc1_w', 'L0_conv_fc1_b', 'L0_conv_fc2_w', 'L0_conv_fc2_b',
        'L1_conv_wq', 'L1_conv_bq', 'L1_conv_wk', 'L1_conv_bk', 'L1_conv_wv', 'L1_conv_bv', 'L1_conv_wo', 'L1_conv_bo']


def kernel(**inputs):
    import numpy as np
    import concourse.bacc as bacc
    from concourse.bass_utils import run_bass_kernel_spmd

    nc = bacc.Bacc("TRN2", target_bir_lowering=False, num_devices=1)
    arrays, args = {}, []
    for name in _INS:
        a = np.ascontiguousarray(inputs[name])
        arrays[f"in_{name}"] = a
        args.append(nc.dram_tensor(f"in_{name}", a.shape, mybir.dt.from_np(a.dtype), kind="ExternalInput").ap())
    args.append(nc.dram_tensor("out", (IMAGES, C, SIDE, SIDE), F32, kind="ExternalOutput").ap())
    build(nc, *args)
    result = run_bass_kernel_spmd(nc, [arrays], core_ids=[0])
    return result.results[0]["out"]
```

```python
from contextlib import ExitStack

import concourse.bass as bass
from concourse import mybir

F32 = mybir.dt.float32
F32R = mybir.dt.float32r
BF16 = mybir.dt.bfloat16
ACT = mybir.ActivationFunctionType
ALU = mybir.AluOpType
AXIS_X = mybir.AxisListType.X

IMAGES, C, SIDE = 8, 128, 32
WIN = 8
KEYS = WIN * WIN
TOKENS = SIDE * SIDE
HALF = TOKENS // 2
WH = HALF // KEYS
PAIRS = WH // 2
HEADS, DH = 8, 16
QUADS = 4
HIDDEN = 256
E = 64
EPS = 1e-5
SCORE_SCALE = DH ** -0.5
VB = DH + 1
Q_, K_, O_, F1_, F2_ = 0, 1, 2, 3, 5


class Loop:

    def __init__(self, eng, i):
        self.eng, self.i, self.kept = eng, i, {}

    def number(self, a, b):
        if isinstance(self.i, int):
            return a * self.i + b
        if (a, b) not in self.kept:
            self.kept[a, b] = self.eng.snap(self.i * a + b)
        return self.kept[a, b]

    def half(self, c):
        return Half(self, c)

    def halves(self, c):
        both = self.number(2, 2 * c + 2)
        return both + 1 if isinstance(self.i, int) and self.i + c == IMAGES - 1 else both

    def image(self, c, times=1):
        return self.number(times, times * (c + 1))

    def follows(self, c):
        return not isinstance(self.i, int) or self.i + c >= 0


class Half:

    tiles, cols, early = range(4), slice(0, HALF), False

    def __init__(self, loop, c):
        self.loop, self.c, self.par = loop, c, c % 2

    def n(self, back=0, times=1):
        return self.loop.number(2 * times, times * (self.c - back + 1))

    def of_parity(self, back=0, times=1):
        return self.loop.number(times, times * ((self.c - back) // 2 + 1))

    def follows(self, back):
        return not isinstance(self.loop.i, int) or 2 * self.loop.i + self.c - back >= 0


class Part(Half):

    def __init__(self, loop, part):
        super().__init__(loop, 1)
        self.part, self.early = part, part == 0
        self.tiles, self.cols = range(2 * part, 2 * part + 2), slice(part * HALF // 2, (part + 1) * HALF // 2)

    def n(self, back=0, times=1):
        return times * (2 * IMAGES - back + (0 if back else self.part))


def build(nc, x, ln1_g, ln1_b, in_w, in_b, out_w, out_b, ln2_g, ln2_b, fc1_w, fc1_b, fc2_w, fc2_b,
          wq, bq, wk, bk, wv, bv, wo, bo, out):
    ctx = ExitStack()
    with ctx:
        def sb(name, shape, dt=F32):
            return ctx.enter_context(nc.sbuf_tensor(name, shape, dt))

        def sem(name):
            return ctx.enter_context(nc.semaphore(name))

        def sems(name, n):
            return [sem(f"{name}{k}") for k in range(n)]

        in_w_rows = sb("in_w_rows", [128, 3, C])
        out_w_rows = sb("out_w_rows", [128, C])
        fc1_rows = sb("fc1_rows", [128, 2, C])
        fc2_rows = sb("fc2_rows", [128, HIDDEN])
        kv_rows = sb("kv_rows", [2 * E, C])
        wo_rows = sb("wo_rows", [C, E])
        wq_rows = sb("wq_rows", [E, C])
        cols = sb("cols", [128, 16])
        G1, B1, G2, B2, INB, OUTB, FC1B, FC2B, BO, BQ = 0, 1, 2, 3, 4, 7, 8, 10, 11, 12
        kv_bias = sb("kv_bias", [128, 2 * E])
        wT = sb("wT", [128, 10, C])
        w_full = sb("w_full", [128, 7, C])
        wh = sb("wh", [128, 7, C], F32R)
        wl = sb("wl", [128, 7, C], F32R)
        wv_cols = sb("wv_cols", [128, C])
        qkv_b = sb("qkv_b", [128, 3])
        fc1_b2 = sb("fc1_b2", [128, 2])
        out_b2 = sb("out_b2", [128, 1])
        head_a = sb("head_a", [128, 2])
        ident = sb("ident", [128, 128])
        neg_ident = sb("neg_ident", [128, 128], BF16)
        minus_half = sb("minus_half", [128, 4])
        table_sink = sb("table_sink", [128, 3])

        x_in = sb("x_in", [C, 2, HALF])
        x_res = sb("x_res", [C, 2, HALF])
        stats1 = sb("stats1", [128, 4, 6])
        mv1 = sb("mv1", [128, 4, 2])
        rstd1 = sb("rstd1", [128, 4])
        xn_tok = sb("xn_tok", [128, 4, C])
        xn = sb("xn", [C, HALF])
        xn_h = sb("xn_h", [C, HALF], F32R)
        xn_l = sb("xn_l", [C, HALF], F32R)
        q_h = sb("q_h", [C, HALF], F32R)
        q_l = sb("q_l", [C, HALF], F32R)
        k_h = sb("k_h", [C, HALF], F32R)
        k_l = sb("k_l", [C, HALF], F32R)
        v_tok = sb("v_tok", [128, PAIRS, C])
        qd_h = sb("qd_h", [C, 2, QUADS, HALF], F32R)
        qd_l = sb("qd_l", [C, 2, QUADS, HALF], F32R)
        kd_h = sb("kd_h", [C, 2, WH, 2, KEYS], F32R)
        kd_l = sb("kd_l", [C, 2, WH, 2, KEYS], F32R)
        vd = sb("vd", [128, 2, WH, 2, VB, QUADS])

        row_max = sb("row_max", [128, 2, HEADS])
        max_wide = sb("max_wide", [128, 2, HEADS, KEYS], BF16)
        probs = sb("probs", [128, 2, 2, QUADS, KEYS])
        inv_sum = sb("inv_sum", [128, HEADS])
        o_tok = sb("o_tok", [128, PAIRS, C])

        o_h = sb("o_h", [C, HALF], F32R)
        o_l = sb("o_l", [C, HALF], F32R)
        y1 = sb("y1", [C, 2, HALF])
        stats2 = sb("stats2", [128, 4, 6])
        mv2 = sb("mv2", [128, 4, 2])
        rstd2 = sb("rstd2", [128, 4])
        yn_tok = sb("yn_tok", [128, 4, C])
        yn_h = sb("yn_h", [C, HALF], F32R)
        yn_l = sb("yn_l", [C, HALF], F32R)
        hid = sb("hid", [128, 2, HALF])
        hid_h = sb("hid_h", [128, 2, HALF], F32R)
        hid_l = sb("hid_l", [128, 2, HALF], F32R)
        y2 = sb("y2", [C, HALF])
        y2_h = sb("y2_h", [C, 2, HALF], F32R)
        y2_l = sb("y2_l", [C, 2, HALF], F32R)
        kv_tok = sb("kv_tok", [128, 2, 4, 2 * E])

        kvT = sb("kvT", [E, E])
        bT = sb("bT", [E, C])
        mT = sb("mT", [C, C])
        m_h = sb("m_h", [C, C], F32R)
        m_l = sb("m_l", [C, C], F32R)
        d_col = sb("d_col", [C, 1])
        out_sb = sb("out_sb", [C, 2, HALF])

        def bank(name):
            return ctx.enter_context(nc.psum_tensor(name, [128, 512], F32))

        p_score = bank("p_score")
        p_scoreT = bank("p_scoreT")
        p_attn = bank("p_attn")
        p_a = [bank("p_a0"), bank("p_a1")]
        p_c = [bank("p_c0"), bank("p_c1")]
        p_d = bank("p_d")

        qkv_w_dma, w_dma = sem("qkv_w_dma"), sem("w_dma")
        ident_set, const_ready = sem("ident_set"), sem("const_ready")
        q_zero_set, v_const_set = sems("q_zero_set", 2), sem("v_const_set")
        wT_ready, wT_kept, bias_ready, bias_kept = sem("wT_ready"), sem("wT_kept"), sem("bias_ready"), sem("bias_kept")
        ob_kept, w_scaled, w_high, w_ready = sem("ob_kept"), sem("w_scaled"), sem("w_high"), sem("w_ready")
        x_dma = sems("x_dma", 2)
        x_res_set = sem("x_res_set")
        xT_ready, ln1_stats, ln1_mv, ln1_var, ln1_rstd, xn_tok_set = (
            sem("xT_ready"), sem("ln1_stats"), sem("ln1_mv"), sem("ln1_var"), sem("ln1_rstd"), sem("xn_tok_set"))
        xnT_ready, xn_high, xn_low, xn_full = sem("xnT_ready"), sem("xn_high"), sem("xn_low"), sem("xn_full")
        q_ready, q_high, q_low, k_ready, k_high, k_low = (
            sem("q_ready"), sem("q_high"), sem("q_low"), sem("k_ready"), sem("k_high"), sem("k_low"))
        v_ready, v_kept = sem("v_ready"), sem("v_kept")
        q_high_dma, q_low_dma, v_dma = sem("q_high_dma"), sem("q_low_dma"), sem("v_dma")
        kd_high, kd_low = sems("kd_high", 2), sems("kd_low", 2)
        score_ready, max_ready, max_wide_ready = sems("score_ready", 4), sems("max_ready", 4), sems("max_wide_ready", 4)
        scoreT_ready, probs_ready = sems("scoreT_ready", 4), sems("probs_ready", 4)
        attn_ready, inv_ready, o_tok_ready = sems("attn_ready", 4), sems("inv_ready", 4), sems("o_tok_ready", 4)
        oT_ready, o_high, o_low, proj_ready, y1_ready = (
            sem("oT_ready"), sem("o_high"), sem("o_low"), sem("proj_ready"), sem("y1_ready"))
        yT_ready, ln2_stats, ln2_mv, ln2_var, ln2_rstd, yn_tok_set = (
            sem("yT_ready"), sem("ln2_stats"), sem("ln2_mv"), sem("ln2_var"), sem("ln2_rstd"), sem("yn_tok_set"))
        ynT_ready, yn_high, yn_low = sem("ynT_ready"), sem("yn_high"), sem("yn_low")
        fc1_ready, hid_high, hid_full, hid_low = sems("fc1_ready", 2), sems("hid_high", 2), sems("hid_full", 2), sems("hid_low", 2)
        fc2_ready, y2_ready, y2_high, y2_low = sem("fc2_ready"), sem("y2_ready"), sem("y2_high"), sem("y2_low")
        kv_ready, kv_kept = sem("kv_ready"), sem("kv_kept")
        kvT_ready, kvT_kept, bT_ready, bT_kept = sem("kvT_ready"), sem("kvT_kept"), sem("bT_ready"), sem("bT_kept")
        mT_ready, mT_kept, m_high, m_low, d_kept = sem("mT_ready"), sem("mT_kept"), sem("m_high"), sem("m_low"), sem("d_kept")
        fin_ready, fin_kept = sems("fin_ready", 2), sems("fin_kept", 2)
        out_dma = sems("out_dma", 2)
        exp_table, silu_table = sem("exp_table"), sem("silu_table")
        pool_waits, pe_waits, dve_waits = sem("pool_waits"), sem("pe_waits"), sem("dve_waits")

        QKV_W_LOADS, W_LOADS = 4, 16

        def col(k, n=1, rows=128):
            return cols[0:rows, k:k + n]

        def in_windows(half, v):
            return half.rearrange("p (v win row c) -> p v win row c", v=2, win=4, row=WIN)[:, v]

        def in_rows(half, v):
            return half.rearrange("p (v row win c) -> p v win row c", v=2, row=WIN, win=4)[:, v]

        def c_banks(h):
            return p_a if h.early else p_c

        def images(eng, prologue, step_even, step_odd, epilogue):
            prologue(Loop(eng, 0))
            first, last = Loop(eng, 0), Loop(eng, IMAGES - 1)
            step_even(first, more=True, c=False)
            step_odd(first, more=True, d=False)
            with eng.Fori(1, IMAGES - 1) as i:
                body = Loop(eng, i)
                step_even(body, more=True, c=True)
                step_odd(body, more=True, d=True)
            step_even(last, more=False, c=True)
            step_odd(last, more=False, d=True)
            epilogue(last)

        block = ctx.enter_context(nc.Block())

        @block.sync
        def _(sp):
            def load(dst, src, done=w_dma):
                sp.dma_start(dst, src).then_inc(done, 16)

            def column(v, n=1):
                return v.rearrange("(n p) -> p n", n=n)

            x_rows = x.rearrange("b c (h row) win -> b h c (row win)", h=2)

            def load_x(h):
                src = x_rows[h.loop.number(1, h.c // 2), h.par]
                if h.follows(2):
                    sp.wait_ge(xT_ready, h.n(2))
                if h.follows(2):
                    sp.wait_ge(x_res_set, h.n(2))
                sp.dma_start(x_in[:, h.par, :], src).then_inc(x_dma[h.par], 16)

            first = Loop(sp, 0)
            load_x(first.half(0))
            load(in_w_rows[:], in_w.rearrange("(n p) c -> p n c", n=3), qkv_w_dma)
            with nc.allow_non_contiguous_dma(reason="biases and gains, one element per partition"):
                load(col(B1), column(ln1_b), qkv_w_dma)
                load(col(G1), column(ln1_g), qkv_w_dma)
                load(col(INB, 3), column(in_b, 3), qkv_w_dma)
            load_x(first.half(1))
            load(out_w_rows[:], out_w)
            load(fc1_rows[:], fc1_w.rearrange("(n p) c -> p n c", n=2))
            load(fc2_rows[:], fc2_w)
            load(kv_rows[0:E, :], wk)
            load(kv_rows[E:2 * E, :], wv)
            load(wo_rows[:], wo)
            load(wq_rows[:], wq)
            with nc.allow_non_contiguous_dma(reason="biases and gains, one element per partition"):
                for k, v, n in ((OUTB, out_b, 1), (G2, ln2_g, 1), (B2, ln2_b, 1), (FC1B, fc1_b, 2), (FC2B, fc2_b, 1),
                                (BO, bo, 1)):
                    load(col(k, n), column(v, n))
                load(col(BQ, rows=E), column(bq))
            load(kv_bias[:, 0:E], bass.AP(bk.tensor, 0, [[0, 128], [1, E]]))
            load(kv_bias[:, E:2 * E], bass.AP(bv.tensor, 0, [[0, 128], [1, E]]))

            def spread_q(h):
                sp.wait_ge(q_high, h.n())
                if h.follows(2):
                    sp.wait_ge(scoreT_ready[PAIRS - 1], h.n(2))
                for j in range(QUADS):
                    head_pair = slice(32 * j, 32 * j + 32)
                    sp.dma_start(qd_h[head_pair, h.par, j, :].bitcast(F32), q_h[head_pair, :].bitcast(F32)
                                 ).then_inc(q_high_dma, 16)
                sp.wait_ge(q_low, h.n())
                for j in range(QUADS):
                    head_pair = slice(32 * j, 32 * j + 32)
                    sp.dma_start(qd_l[head_pair, h.par, j, :].bitcast(F32), q_l[head_pair, :].bitcast(F32)
                                 ).then_inc(q_low_dma, 16)

            def spread_v(h):
                sp.wait_ge(v_kept, h.n())
                if h.follows(2):
                    sp.wait_ge(attn_ready[PAIRS - 1], h.n(2))
                slot = vd[:, h.par].rearrange("row (p win) a d j -> row p win a (d j)", win=2)
                for a in range(2):
                    for win in range(2):
                        sp.dma_start(slot[64 * a:64 * a + 64, :, win, a, 0:KEYS],
                                     v_tok[64 * win:64 * win + 64, :, 64 * a:64 * a + 64]).then_inc(v_dma, 16)

            def store(loop, c):
                for half in range(2):
                    dst = out.rearrange("b c (h row) win -> b h c (row win)", h=2)[loop.number(1, c), half]
                    sp.wait_ge(fin_kept[half], loop.image(c))
                    sp.dma_start(dst, out_sb[:, half, :]).then_inc(out_dma[half], 16)

            def prologue(loop):
                sp.wait_ge(q_zero_set[0], 2)
                spread_q(loop.half(0))
                sp.wait_ge(v_const_set, 5)
                spread_v(loop.half(0))
                sp.wait_ge(q_zero_set[1], 2)

            def step_even(loop, more, c):
                if more:
                    load_x(loop.half(2))
                spread_q(loop.half(1))
                spread_v(loop.half(1))

            def step_odd(loop, more, d):
                if more:
                    load_x(loop.half(3))
                    spread_q(loop.half(2))
                    spread_v(loop.half(2))
                if d:
                    store(loop, -1)

            def epilogue(loop):
                store(loop, 0)
                for half in range(2):
                    sp.wait_ge(out_dma[half], 16 * IMAGES)

            images(sp, prologue, step_even, step_odd, epilogue)

        @block.gpsimd
        def _(pool):
            pool.memset(ident[:], 0.0).then_inc(ident_set, 1)
            pool.wait_ge(ident_set, 1)
            pool.affine_select(out=ident[:], in_=ident[:], compare_op=ALU.not_equal, fill=1.0, base=0,
                               pattern=[[-1, 128]], channel_multiplier=1).then_inc(ident_set, 1)
            pool.wait_ge(ident_set, 2)
            pool.tensor_scalar(neg_ident[:], ident[:], -1.0, None, ALU.mult).then_inc(const_ready, 1)
            pool.memset(minus_half[:], -0.5).then_inc(const_ready, 1)
            pool.memset(vd[:], 0.0).then_inc(v_const_set, 1)
            pool.wait_ge(v_const_set, 1)
            for a in range(2):
                for s in range(2):
                    pool.memset(vd[64 * a:64 * a + 64, s, :, a, DH, :], 1.0).then_inc(v_const_set, 1)
            pool.wait_ge(v_const_set, 5)

            def waited():
                pool.sem_inc(pool_waits, 1)

            def residual(h):
                pool.wait_ge(x_dma[h.par], h.of_parity(times=16))
                if h.follows(2):
                    pool.wait_ge(y1_ready, h.n(2))
                waited()
                for v in range(2):
                    last = pool.tensor_scalar(in_windows(x_res[:, h.par, :], v), in_rows(x_in[:, h.par, :], v),
                                              out_b2[:, 0:1], None, ALU.add)
                last.then_inc(x_res_set, 1)

            def rstd(h, mv, mv_set, var_set, out_, out_set, read):
                pool.wait_ge(mv_set, h.n())
                if h.follows(1):
                    pool.wait_ge(read, h.n(1))
                waited()
                tiles = slice(h.tiles[0], h.tiles[-1] + 1)
                pool.tensor_scalar(out_[:, tiles], mv[:, tiles, 1], EPS, None, ALU.add).then_inc(var_set, 1)
                pool.wait_ge(var_set, h.n())
                pool.tensor_tensor(out_[:, tiles], out_[:, tiles], minus_half[:, tiles], ALU.pow).then_inc(out_set, 1)

            def k_low_block(h):
                if h.follows(2):
                    pool.wait_ge(scoreT_ready[PAIRS - 1], h.n(2))
                pool.wait_ge(k_low, h.n())
                waited()
                pool.tensor_scalar(kd_l[:, h.par, :, 0, :], k_l[:].bitcast(F32).rearrange("p (win k) -> p win k", k=KEYS),
                                   head_a[:, 0:1], None, ALU.mult).then_inc(kd_low[0], 1)

            def hidden_low(h, t):
                pool.wait_ge(hid_high[t], h.n())
                pool.wait_ge(hid_full[t], h.n())
                if h.follows(1):
                    pool.wait_ge(fc2_ready, h.n(1))
                pool.tensor_tensor(hid_l[:, t], hid[:, t], hid_h[:, t].bitcast(F32), ALU.subtract
                                   ).then_inc(hid_low[t], 1)

            def y2_low_part(h):
                pool.wait_ge(y2_high, h.n())
                pool.tensor_tensor(y2_l[:, h.par, h.cols], y2[:, h.cols], y2_h[:, h.par, h.cols].bitcast(F32), ALU.subtract
                                   ).then_inc(y2_low, 1)

            def rstd1_of(h):
                rstd(h, mv1, ln1_mv, ln1_var, rstd1, ln1_rstd, xn_tok_set)

            def rstd2_of(h):
                rstd(h, mv2, ln2_mv, ln2_var, rstd2, ln2_rstd, yn_tok_set)

            def prologue(loop):
                rstd1_of(loop.half(0))
                pool.memset(qd_h[:, 1].bitcast(F32), 0.0).then_inc(q_zero_set[1], 1)
                pool.memset(qd_l[:, 1].bitcast(F32), 0.0).then_inc(q_zero_set[1], 1)
                k_low_block(loop.half(0))
                rstd1_of(loop.half(1))
                pool.wait_ge(ob_kept, 1)
                residual(loop.half(0))

            def step(loop, b, with_a, with_next, with_c, with_tail, with_last=False):
                a, next_a, c, tail = loop.half(b.c + 1), loop.half(b.c + 2), loop.half(b.c - 1), loop.half(b.c - 2)
                if with_tail:
                    y2_low_part(tail)
                if with_c:
                    rstd2_of(c)
                if with_a:
                    residual(a)
                    k_low_block(a)
                if with_next:
                    rstd1_of(next_a)
                if with_c:
                    hidden_low(c, 0)
                if with_last:
                    rstd2_of(Part(loop, 0))
                if with_c:
                    hidden_low(c, 1)

            def step_even(loop, more, c):
                step(loop, loop.half(0), True, more, c, c)

            def step_odd(loop, more, d):
                step(loop, loop.half(1), more, more, True, d, not more)

            def epilogue(loop):
                early, late = Part(loop, 0), Part(loop, 1)
                rstd2_of(late)
                y2_low_part(loop.half(0))
                y2_low_part(early)
                y2_low_part(late)

            images(pool, prologue, step_even, step_odd, epilogue)

        @block.tensor
        def _(pe):
            def three_passes(dst, blocks, moving):
                passes = [(weight, moving_part) for (b_h, b_l), (m_h, m_l) in zip(blocks, moving)
                          for weight, moving_part in ((b_h, m_h), (b_h, m_l), (b_l, m_h))]
                for k, (weight, moving_part) in enumerate(passes):
                    last = pe.matmul(dst, weight, moving_part, start=k == 0, stop=k == len(passes) - 1)
                return last

            def weights(b):
                return wh[:, b, :], wl[:, b, :]

            def load_qkv_weights():
                pe.wait_ge(qkv_w_dma, 16 * QKV_W_LOADS)
                for k in range(3):
                    last = pe.transpose(p_score[:, C * k:C * k + C], in_w_rows[:, k, :], ident[:])
                last.then_inc(wT_ready, 1)
                pe.wait_ge(wT_kept, 1)
                for k in range(3):
                    last = pe.matmul(p_d[:, k:k + 1], wT[:, k, :], col(B1), start=True, stop=True)
                last.then_inc(bias_ready, 1)

            def load_weights():
                pe.wait_ge(w_dma, 16 * W_LOADS)
                blocks = [out_w_rows[:]] + [fc1_rows[:, k, :] for k in range(2)] + \
                         [fc2_rows[:, 0:C], fc2_rows[:, C:2 * C]] + [kv_rows[:]]
                for k, weight in enumerate(blocks):
                    pe.transpose(p_c[k // 4][:, C * (k % 4):C * (k % 4) + C], weight, ident[:])
                pe.transpose(p_c[1][0:E, 2 * C:3 * C], wo_rows[:], ident[:]).then_inc(wT_ready, 1)

            def load_biases():
                pe.wait_ge(wT_kept, 2)
                pe.wait_ge(bias_kept, 1)
                for k in range(2):
                    pe.matmul(p_d[:, 3 + k:4 + k], wT[:, 4 + k, :], col(B2), start=True, stop=True)
                pe.matmul(p_d[:, 8:9], wT[:, 3, :], qkv_b[:, 2:3], start=True, stop=True).then_inc(bias_ready, 1)

            def a_transpose(h):
                pe.wait_ge(x_dma[h.par], h.of_parity(times=16))
                if h.follows(1):
                    pe.wait_ge(v_kept, h.n(1))
                for t in range(4):
                    last = pe.transpose(p_a[0][:, C * t:C * t + C], x_in[:, h.par, C * t:C * t + C], ident[:])
                last.then_inc(xT_ready, 1)

            def a_back(h):
                pe.wait_ge(xn_tok_set, h.n())
                if h.follows(1):
                    pe.wait_ge(k_high, h.n(1))
                if h.follows(1):
                    pe.wait_ge(k_low, h.n(1))
                for t in range(4):
                    last = pe.transpose(p_a[1][:, C * t:C * t + C], xn_tok[:, t, :], ident[:])
                last.then_inc(xnT_ready, 1)

            def a_q(h):
                pe.wait_ge(xn_high, h.n())
                pe.wait_ge(xn_low, h.n())
                three_passes(p_a[0][:], [weights(Q_)], [(xn_h[:], xn_l[:])]).then_inc(q_ready, 1)

            def a_k(h):
                pe.wait_ge(xn_full, h.n())
                three_passes(p_a[1][:], [weights(K_)], [(xn_h[:], xn_l[:])]).then_inc(k_ready, 1)

            def a_v(h):
                pe.wait_ge(q_high, h.n())
                pe.wait_ge(q_low, h.n())
                for p in range(PAIRS):
                    last = pe.matmul(p_a[0][:, C * p:C * p + C], xn[:, C * p:C * p + C], wv_cols[:],
                                     start=True, stop=True)
                last.then_inc(v_ready, 1)

            def b_score(h, p):
                if p == 0:
                    pe.wait_ge(q_high_dma, h.n(times=16 * QUADS))
                    pe.wait_ge(kd_high[0], h.n())
                    pe.wait_ge(kd_high[1], h.n())
                    if h.follows(1):
                        pe.wait_ge(max_ready[PAIRS - 1], h.n(1))
                else:
                    pe.wait_ge(max_ready[p - 1], h.n())
                for j in range(QUADS):
                    for win, rows in ((1, 2 * KEYS), (0, KEYS)):
                        last = pe.matmul(p_score[0:rows, 2 * KEYS * j:2 * KEYS * (j + 1)],
                                         qd_h[:, h.par, j, 2 * KEYS * p:2 * KEYS * p + rows],
                                         kd_h[:, h.par, 2 * p + win], start=True, stop=True)
                last.then_inc(score_ready[p], 1)

            def b_scoreT(h, p):
                pe.wait_ge(max_wide_ready[p], h.n())
                if p == 0:
                    pe.wait_ge(q_low_dma, h.n(times=16 * QUADS))
                    pe.wait_ge(kd_low[0], h.n())
                    pe.wait_ge(kd_low[1], h.n())
                    if h.follows(1):
                        pe.wait_ge(probs_ready[PAIRS - 1], h.n(1))
                else:
                    pe.wait_ge(probs_ready[p - 1], h.n())
                dst = p_scoreT[:].rearrange("row (win j q) -> row win j q", win=2, j=QUADS)
                for j in range(QUADS):
                    pe.matmul(dst[:, :, j, :], max_wide[:, p % 2, 2 * j:2 * j + 2, :],
                              neg_ident[:], start=j == 0, stop=False, skip_group_check=True)
                for win in range(2):
                    window = 2 * p + win
                    for k, (kd, qd) in enumerate(((kd_h, qd_h), (kd_h, qd_l), (kd_l, qd_h))):
                        last = pe.matmul(dst[:, win], kd[:, h.par, window], qd[:, h.par, :, KEYS * window:KEYS * (window + 1)],
                                         start=False, stop=win == 1 and k == 2, skip_group_check=True)
                last.then_inc(scoreT_ready[p], 1)

            def b_attn(h, p):
                pe.wait_ge(probs_ready[p], h.n())
                if p == 0:
                    pe.wait_ge(v_dma, h.n(times=16 * 4))
                    if h.follows(1):
                        pe.wait_ge(o_tok_ready[PAIRS - 1], h.n(1))
                else:
                    pe.wait_ge(o_tok_ready[p - 1], h.n())
                for win in range(2):
                    for j in range(QUADS):
                        last = pe.matmul(p_attn[64 * win:64 * win + 64, 2 * VB * j:2 * VB * (j + 1)],
                                         probs[:, p % 2, win, j, :],
                                         vd[:, h.par, 2 * p + win, :, :, j].rearrange("row a d -> row (a d)"),
                                         start=True, stop=True)
                last.then_inc(attn_ready[p], 1)

            def c_transpose(h):
                pe.wait_ge(o_tok_ready[h.tiles[-1]], h.loop.half(h.c).n())
                if h.early:
                    pe.wait_ge(v_kept, 2 * IMAGES)
                    pe.wait_ge(k_low, 2 * IMAGES)
                elif h.follows(1):
                    pe.wait_ge(hid_high[0], h.n(1))
                    pe.wait_ge(hid_full[0], h.n(1))
                for t in h.tiles:
                    last = pe.transpose(c_banks(h)[0][:, C * t:C * t + C], o_tok[:, t, :], ident[:])
                last.then_inc(oT_ready, 1)

            def c_project(h):
                pe.wait_ge(o_high, h.n())
                pe.wait_ge(o_low, h.n())
                pe.wait_ge(w_ready, 2)
                three_passes(c_banks(h)[0][:, h.cols], [weights(O_)], [(o_h[:, h.cols], o_l[:, h.cols])]
                             ).then_inc(proj_ready, 1)

            def c_yT(h):
                pe.wait_ge(y1_ready, h.n())
                for t in h.tiles:
                    last = pe.transpose(c_banks(h)[0][:, C * t:C * t + C], y1[:, h.par, C * t:C * t + C], ident[:])
                last.then_inc(yT_ready, 1)

            def c_back(h):
                pe.wait_ge(yn_tok_set, h.n())
                for t in h.tiles:
                    last = pe.transpose(c_banks(h)[0][:, C * t:C * t + C], yn_tok[:, t, :], ident[:])
                last.then_inc(ynT_ready, 1)

            def c_fc1(h, t):
                pe.wait_ge(yn_high, h.n())
                pe.wait_ge(yn_low, h.n())
                if t == 1 and not h.early:
                    if h.follows(1):
                        pe.wait_ge(kv_kept, h.n(1))
                three_passes(c_banks(h)[t][:, h.cols], [weights(F1_ + t)], [(yn_h[:, h.cols], yn_l[:, h.cols])]
                             ).then_inc(fc1_ready[t], 1)

            def c_fc2(h):
                pe.wait_ge(hid_high[0], h.n())
                pe.wait_ge(hid_low[0], h.n())
                pe.wait_ge(hid_high[1], h.n())
                pe.wait_ge(hid_low[1], h.n())
                three_passes(c_banks(h)[1][:, h.cols], [weights(F2_), weights(F2_ + 1)],
                             [(hid_h[:, t, h.cols], hid_l[:, t, h.cols]) for t in range(2)]).then_inc(fc2_ready, 1)

            def c_kv(h):
                pe.wait_ge(y2_ready, h.n())
                for t in h.tiles:
                    last = pe.matmul(c_banks(h)[1][:, C * t:C * t + C], y2[:, C * t:C * t + C], wT[:, 8, :],
                                     start=True, stop=True)
                last.then_inc(kv_ready, 1)

            def d_kvT(loop, c, tiles=range(8)):
                pe.wait_ge(kv_kept, loop.halves(c) - 1 if tiles[-1] < 7 else loop.halves(c))
                if loop.follows(c - 1):
                    pe.wait_ge(fin_kept[1], loop.image(c - 1))
                for n in tiles:
                    tile = kv_tok[:, n // 4, n % 4]
                    last = pe.matmul(p_d[0:E, 0:E], tile[:, E:2 * E], tile[:, 0:E], start=n == 0, stop=n == 7)
                if tiles[-1] == 7:
                    last.then_inc(kvT_ready, 1)

            def d_bT(loop, c):
                pe.wait_ge(kvT_kept, loop.image(c))
                pe.sem_inc(pe_waits, 1)
                pe.matmul(p_d[0:E, 0:C], kvT[:], wT[0:E, 9, :], start=True, stop=True).then_inc(bT_ready, 1)

            def d_mT(loop, c):
                pe.wait_ge(bT_kept, loop.image(c))
                pe.matmul(p_d[:, 0:C], wq_rows[:], bT[:], start=True, stop=True)
                pe.matmul(p_d[:, C:C + 1], bT[:], col(BQ, rows=E), start=True, stop=True).then_inc(mT_ready, 1)

            def d_final(loop, c, half, dst):
                if half == 0:
                    pe.wait_ge(m_high, loop.image(c))
                    pe.wait_ge(m_low, loop.image(c))
                    pe.wait_ge(d_kept, loop.image(c))
                    pe.wait_ge(y2_low, loop.halves(c))
                elif dst is p_d:
                    pe.wait_ge(fin_kept[0], loop.image(c))
                three_passes(dst[:], [(m_h[:], m_l[:])], [(y2_h[:, half], y2_l[:, half])]
                             ).then_inc(fin_ready[half], 1)

            def prologue(loop):
                a = loop.half(0)
                pe.wait_ge(ident_set, 2)
                a_transpose(a)
                load_qkv_weights()
                a_back(a)
                pe.wait_ge(w_ready, 1)
                a_q(a)
                a_k(a)
                a_v(a)
                load_weights()
                a_transpose(loop.half(1))
                load_biases()
                pe.wait_ge(const_ready, 4)

            def step(loop, b, with_a, with_next, with_c, with_tail, with_d, with_last=False):
                a, next_a, c, tail = loop.half(b.c + 1), loop.half(b.c + 2), loop.half(b.c - 1), loop.half(b.c - 2)
                b_score(b, 0)
                if with_a and with_c:
                    a_back(a)
                if with_c:
                    c_transpose(c)
                b_score(b, 1)
                b_scoreT(b, 0)
                if not with_c:
                    a_back(a)
                if with_c:
                    c_project(c)
                b_score(b, 2)
                if with_tail:
                    c_fc2(tail)
                b_attn(b, 0)
                if with_c:
                    c_yT(c)
                if with_a:
                    a_q(a)
                if with_tail:
                    c_kv(tail)
                b_scoreT(b, 1)
                b_score(b, 3)
                if with_d:
                    d_kvT(loop, -1)
                if with_a:
                    a_k(a)
                b_attn(b, 1)
                if with_a:
                    a_v(a)
                if with_d:
                    d_bT(loop, -1)
                b_scoreT(b, 2)
                if with_d:
                    d_mT(loop, -1)
                if with_next:
                    a_transpose(next_a)
                if with_c:
                    c_back(c)
                if with_last:
                    c_transpose(Part(loop, 0))
                b_attn(b, 2)
                if with_d:
                    d_final(loop, -1, 0, p_d)
                b_scoreT(b, 3)
                if with_last:
                    c_project(Part(loop, 0))
                if with_c:
                    c_fc1(c, 0)
                    c_fc1(c, 1)
                if with_d:
                    d_final(loop, -1, 1, p_d)
                b_attn(b, 3)

            def step_even(loop, more, c):
                step(loop, loop.half(0), True, more, c, c, False)

            def step_odd(loop, more, d):
                step(loop, loop.half(1), more, more, True, d, d, not more)

            def epilogue(loop):
                early, late = Part(loop, 0), Part(loop, 1)
                c_yT(early)
                c_transpose(late)
                c_project(late)
                c_back(early)
                c_yT(late)
                c_fc2(loop.half(0))
                c_fc1(early, 0)
                c_fc1(early, 1)
                c_kv(loop.half(0))
                c_back(late)
                c_fc2(early)
                c_fc1(late, 0)
                c_fc1(late, 1)
                c_kv(early)
                c_fc2(late)
                d_kvT(loop, 0, range(6))
                c_kv(late)
                d_kvT(loop, 0, range(6, 8))
                d_bT(loop, 0)
                d_mT(loop, 0)
                d_final(loop, 0, 0, p_d)
                pe.wait_ge(v_kept, 2 * IMAGES)
                d_final(loop, 0, 1, p_a[0])

            images(pe, prologue, step_even, step_odd, epilogue)

        @block.scalar
        def _(act):
            def load_exp_table(h):
                if h.follows(1):
                    act.wait_ge(exp_table, h.n(1))
                act.activation(table_sink[:, 0:1], ident[:, 0:1], ACT.Exp).then_inc(exp_table, 1)

            def load_silu_table(h):
                if h.follows(1):
                    act.wait_ge(silu_table, h.n(1))
                act.activation(table_sink[:, 1:2], ident[:, 0:1], ACT.Silu).then_inc(silu_table, 1)

            def a_xn(h):
                act.wait_ge(xnT_ready, h.n())
                if h.follows(1):
                    act.wait_ge(q_ready, h.n(1))
                if h.follows(1):
                    act.wait_ge(v_ready, h.n(1))
                for dst, done in ((xn_h, xn_high), (xn, xn_full)):
                    for v in range(2):
                        last = act.activation(in_windows(dst[:], v), in_rows(p_a[1][:], v), ACT.Copy)
                    last.then_inc(done, 1)

            def a_q(h):
                act.wait_ge(q_ready, h.n())
                if h.follows(1):
                    act.wait_ge(q_high_dma, h.n(1, times=16 * QUADS))
                act.activation(q_h[:], p_a[0][:], ACT.Identity, bias=qkv_b[:, 0:1]).then_inc(q_high, 1)

            def a_k(h):
                act.wait_ge(k_ready, h.n())
                if h.follows(1):
                    act.wait_ge(kd_high[0], h.n(1))
                if h.follows(1):
                    act.wait_ge(kd_high[1], h.n(1))
                act.activation(k_h[:], p_a[1][:], ACT.Identity, bias=qkv_b[:, 1:2]).then_inc(k_high, 1)

            def a_k_block(h, a):
                if h.follows(2):
                    act.wait_ge(scoreT_ready[PAIRS - 1], h.n(2))
                act.wait_ge(k_high, h.n())
                act.activation(kd_h[:, h.par, :, a, :], k_h[:].bitcast(F32).rearrange("p (win k) -> p win k", k=KEYS),
                               ACT.Copy, scale=head_a[:, a:a + 1]).then_inc(kd_high[a], 1)

            def a_v(h):
                act.wait_ge(v_ready, h.n())
                if h.follows(1):
                    act.wait_ge(v_dma, h.n(1, times=16 * 4))
                act.activation(v_tok[:], p_a[0][:], ACT.Copy).then_inc(v_kept, 1)

            def b_exp(h, p):
                act.wait_ge(scoreT_ready[p], h.n())
                if p < 2:
                    if h.follows(1):
                        act.wait_ge(attn_ready[p + 2], h.n(1))
                else:
                    act.wait_ge(attn_ready[p - 2], h.n())
                act.activation(probs[:, p % 2], p_scoreT[:].rearrange("row (win j q) -> row win j q", win=2, j=QUADS),
                               ACT.Exp, scale=SCORE_SCALE).then_inc(probs_ready[p], 1)

            def b_widen(h, p):
                act.wait_ge(max_ready[p], h.n())
                act.wait_ge(scoreT_ready[p - 2], h.n())
                act.activation(max_wide[:, p % 2], row_max[:, p % 2].unsqueeze(2).to_broadcast([128, HEADS, KEYS]),
                               ACT.Copy).then_inc(max_wide_ready[p], 1)

            def c_y2(h):
                act.wait_ge(y2_ready, h.n())
                if h.follows(2):
                    act.wait_ge(fin_ready[h.par], h.of_parity(2))
                act.activation(y2_h[:, h.par, h.cols], y2[:, h.cols], ACT.Copy).then_inc(y2_high, 1)

            def c_o(h):
                act.wait_ge(oT_ready, h.n())
                if h.follows(1):
                    act.wait_ge(proj_ready, h.n(1))
                act.activation(o_h[:, h.cols], c_banks(h)[0][:, h.cols], ACT.Copy).then_inc(o_high, 1)

            def c_yn(h):
                act.wait_ge(ynT_ready, h.n())
                if h.follows(1):
                    act.wait_ge(fc1_ready[1], h.n(1))
                act.activation(yn_h[:, h.cols], c_banks(h)[0][:, h.cols], ACT.Copy).then_inc(yn_high, 1)

            def c_silu(h, t):
                act.wait_ge(fc1_ready[t], h.n())
                if h.follows(1):
                    act.wait_ge(fc2_ready, h.n(1))
                if h.follows(1):
                    act.wait_ge(hid_low[t], h.n(1))
                act.activation(hid_h[:, t, h.cols], c_banks(h)[t][:, h.cols], ACT.Silu, bias=fc1_b2[:, t:t + 1]
                               ).then_inc(hid_high[t], 1)
                act.activation(hid[:, t, h.cols], c_banks(h)[t][:, h.cols], ACT.Silu, bias=fc1_b2[:, t:t + 1]
                               ).then_inc(hid_full[t], 1)

            def d_out(loop, c, half):
                act.wait_ge(fin_ready[half], loop.image(c))
                if loop.follows(c - 1):
                    act.wait_ge(out_dma[half], loop.image(c - 1, times=16))
                for v in range(2):
                    last = act.activation(in_rows(out_sb[:, half, :], v), in_windows(p_d[:], v), ACT.Identity,
                                          bias=d_col[:, 0:1])
                last.then_inc(fin_kept[half], 1)

            def prologue(loop):
                a = loop.half(0)
                act.wait_ge(ident_set, 2)
                act.activation(table_sink[:, 2:3], ident[:, 0:1], ACT.Exp)
                a_xn(a)
                act.wait_ge(const_ready, 4)
                act.wait_ge(bias_kept, 1)
                a_q(a)
                a_k(a)
                a_k_block(a, 0)
                a_k_block(a, 1)
                a_v(a)

            def step(loop, b, with_a, with_next, with_c, with_tail, with_d, with_last=False):
                a, next_a, c, tail = loop.half(b.c + 1), loop.half(b.c + 2), loop.half(b.c - 1), loop.half(b.c - 2)
                load_exp_table(b)
                if with_a:
                    a_xn(a)
                b_exp(b, 0)
                b_widen(b, 2)
                if with_tail:
                    c_y2(tail)
                if with_a:
                    a_q(a)
                b_exp(b, 1)
                if with_a:
                    a_k(a)
                    a_k_block(a, 0)
                    a_v(a)
                b_exp(b, 2)
                if with_c:
                    c_yn(c)
                if with_last:
                    c_o(Part(loop, 0))
                if with_a:
                    a_k_block(a, 1)
                if with_d:
                    d_out(loop, -1, 0)
                b_exp(b, 3)
                load_silu_table(b)
                if with_c:
                    c_silu(c, 0)
                    c_silu(c, 1)
                if not with_last:
                    c_o(b)
                if with_d and not with_last:
                    d_out(loop, -1, 1)

            def step_even(loop, more, c):
                step(loop, loop.half(0), True, more, c, c, False)

            def step_odd(loop, more, d):
                step(loop, loop.half(1), more, more, True, d, d, not more)

            def epilogue(loop):
                early, late = Part(loop, 0), Part(loop, 1)
                c_o(late)
                d_out(loop, -1, 1)
                c_yn(early)
                c_y2(loop.half(0))
                c_silu(early, 0)
                c_silu(early, 1)
                c_yn(late)
                c_silu(late, 0)
                c_silu(late, 1)
                c_y2(early)
                c_y2(late)
                d_out(loop, 0, 0)

            images(act, prologue, step_even, step_odd, epilogue)

        @block.vector
        def _(dve):
            dve.memset(qd_h[:, 0].bitcast(F32), 0.0).then_inc(q_zero_set[0], 1)
            dve.memset(qd_l[:, 0].bitcast(F32), 0.0).then_inc(q_zero_set[0], 1)

            def load_qkv_weights():
                dve.wait_ge(wT_ready, 1)
                dve.tensor_copy(wT[:, 0:3, :], p_score[:, 0:3 * C]).then_inc(wT_kept, 1)
                dve.wait_ge(wT_kept, 1)
                dve.tensor_scalar(w_full[:, Q_:K_ + 1, :], wT[:, 0:2, :], col(G1), None, ALU.mult)
                dve.tensor_scalar(wv_cols[:].rearrange("p (a d j) -> p a d j", a=2, d=DH),
                                  wT[:, 2, :].rearrange("p (j a d) -> p a d j", j=QUADS, a=2), col(G1), None, ALU.mult
                                  ).then_inc(w_scaled, 1)
                dve.wait_ge(w_scaled, 1)
                dve.tensor_copy(wh[:, 0:2], w_full[:, 0:2]).then_inc(w_high, 1)
                dve.wait_ge(w_high, 1)
                dve.tensor_tensor(wl[:, 0:2], w_full[:, 0:2], wh[:, 0:2].bitcast(F32), ALU.subtract
                                  ).then_inc(w_ready, 1)

            def load_qkv_biases():
                dve.wait_ge(bias_ready, 1)
                dve.tensor_tensor(qkv_b[:], p_d[:, 0:3], col(INB, 3), ALU.add).then_inc(bias_kept, 1)

            def load_weights():
                dve.wait_ge(wT_ready, 2)
                dve.tensor_copy(wT[:, 3:7, :], p_c[0][:])
                dve.tensor_copy(wT[0:E, 9, :], p_c[1][0:E, 2 * C:3 * C])
                dve.tensor_copy(wT[:, 7:9, :], p_c[1][:, 0:2 * C]).then_inc(wT_kept, 1)

            def load_biases():
                dve.wait_ge(bias_ready, 2)
                dve.tensor_tensor(fc1_b2[:], p_d[:, 3:5], col(FC1B, 2), ALU.add)
                dve.tensor_tensor(out_b2[:], p_d[:, 8:9], col(OUTB), ALU.add).then_inc(ob_kept, 1)

            def head_columns():
                dve.wait_ge(ident_set, 2)
                heads = ident[:].rearrange("p (j a d) -> p a j d", j=QUADS, a=2)
                for a in range(2):
                    dve.tensor_reduce(head_a[:, a:a + 1], heads[:, a], mybir.AxisListType.XY, ALU.add
                                      ).then_inc(const_ready, 1)

            def split_weights():
                dve.wait_ge(wT_kept, 2)
                dve.tensor_copy(w_full[:, O_, :], wT[:, 3, :])
                dve.tensor_scalar(w_full[:, F1_:F1_ + 2, :], wT[:, 4:6, :], col(G2), None, ALU.mult)
                dve.tensor_copy(w_full[:, F2_:F2_ + 2, :], wT[:, 6:8, :]).then_inc(w_scaled, 1)
                dve.wait_ge(w_scaled, 2)
                dve.tensor_copy(wh[:, 2:7], w_full[:, 2:7]).then_inc(w_high, 1)
                dve.wait_ge(w_high, 2)
                dve.tensor_tensor(wl[:, 2:7], w_full[:, 2:7], wh[:, 2:7].bitcast(F32), ALU.subtract
                                  ).then_inc(w_ready, 1)

            def statistics(h, src, ready, stats, stats_set):
                dve.wait_ge(ready, h.n())
                for t in h.tiles:
                    last = dve.bn_stats(stats[:, t, :], src[:, C * t:C * t + C])
                last.then_inc(stats_set, 1)

            def aggregate(h, stats, stats_set, mv, mv_set, read):
                if h.follows(1):
                    dve.wait_ge(read, h.n(1))
                dve.wait_ge(stats_set, h.n())
                dve.sem_inc(dve_waits, 1)
                for t in h.tiles:
                    last = dve.bn_aggr(mv[:, t, :], stats[:, t, :])
                last.then_inc(mv_set, 1)

            def normalise(h, dst, src, mv, rstd, rstd_set, done, read):
                dve.wait_ge(rstd_set, h.n())
                if h.follows(1):
                    dve.wait_ge(read, h.n(1))
                for t in h.tiles:
                    last = dve.tensor_scalar(dst[:, t, :], src[:, C * t:C * t + C], mv[:, t, 0:1], rstd[:, t:t + 1],
                                             ALU.subtract, ALU.mult)
                last.then_inc(done, 1)

            def a_stats(h):
                statistics(h, p_a[0], xT_ready, stats1, ln1_stats)

            def a_aggregate(h):
                aggregate(h, stats1, ln1_stats, mv1, ln1_mv, xn_tok_set)

            def a_norm(h):
                normalise(h, xn_tok, p_a[0], mv1, rstd1, ln1_rstd, xn_tok_set, xnT_ready)

            def a_xn(h):
                dve.wait_ge(xn_full, h.n())
                if h.follows(1):
                    dve.wait_ge(k_ready, h.n(1))
                for v in range(2):
                    last = dve.tensor_tensor(in_windows(xn_l[:], v), in_rows(p_a[1][:], v),
                                             in_windows(xn_h[:].bitcast(F32), v), ALU.subtract)
                last.then_inc(xn_low, 1)

            def a_q(h):
                dve.wait_ge(q_high, h.n())
                if h.follows(1):
                    dve.wait_ge(q_low_dma, h.n(1, times=16 * QUADS))
                dve.scalar_tensor_tensor(q_l[:], p_a[0][:], qkv_b[:, 0:1], q_h[:].bitcast(F32),
                                         ALU.add, ALU.subtract).then_inc(q_low, 1)

            def a_k(h):
                dve.wait_ge(k_high, h.n())
                if h.follows(1):
                    dve.wait_ge(kd_low[0], h.n(1))
                if h.follows(1):
                    dve.wait_ge(kd_low[1], h.n(1))
                dve.scalar_tensor_tensor(k_l[:], p_a[1][:], qkv_b[:, 1:2], k_h[:].bitcast(F32),
                                         ALU.add, ALU.subtract).then_inc(k_low, 1)

            def a_k_low_block(h):
                if h.follows(2):
                    dve.wait_ge(scoreT_ready[PAIRS - 1], h.n(2))
                dve.wait_ge(k_low, h.n())
                dve.tensor_scalar(kd_l[:, h.par, :, 1, :], k_l[:].bitcast(F32).rearrange("p (win k) -> p win k", k=KEYS),
                                  head_a[:, 1:2], None, ALU.mult).then_inc(kd_low[1], 1)

            def b_max(h, p):
                dve.wait_ge(score_ready[p], h.n())
                if p < 2:
                    if h.follows(1):
                        dve.wait_ge(max_wide_ready[p + 2], h.n(1))
                else:
                    dve.wait_ge(max_wide_ready[p - 2], h.n())
                dve.tensor_reduce(row_max[:, p % 2], p_score[:].rearrange("row (h k) -> row h k", h=HEADS), AXIS_X, ALU.max
                                  ).then_inc(max_ready[p], 1)

            def b_widen(h, p):
                dve.wait_ge(max_ready[p], h.n())
                if p < 2:
                    if h.follows(1):
                        dve.wait_ge(scoreT_ready[p + 2], h.n(1))
                else:
                    dve.wait_ge(scoreT_ready[p - 2], h.n())
                dve.tensor_copy(max_wide[:, p % 2], row_max[:, p % 2].unsqueeze(2).to_broadcast([128, HEADS, KEYS])
                                ).then_inc(max_wide_ready[p], 1)

            def b_norm(h, p):
                dve.wait_ge(attn_ready[p], h.n())
                if p == 0:
                    if h.follows(1):
                        dve.wait_ge(oT_ready, h.n(1))
                heads = p_attn[:, 0:HEADS * VB].rearrange("row (h d) -> row h d", h=HEADS)
                dve.reciprocal(inv_sum[:], heads[:, :, DH]).then_inc(inv_ready[p], 1)
                dve.wait_ge(inv_ready[p], h.n())
                dve.tensor_tensor(o_tok[:, p, :].rearrange("row (h d) -> row h d", h=HEADS), heads[:, :, 0:DH],
                                  inv_sum[:].unsqueeze(2).to_broadcast([128, HEADS, DH]), ALU.mult
                                  ).then_inc(o_tok_ready[p], 1)

            def c_o(h):
                dve.wait_ge(o_high, h.n())
                if h.follows(1):
                    dve.wait_ge(proj_ready, h.n(1))
                dve.tensor_tensor(o_l[:, h.cols], c_banks(h)[0][:, h.cols], o_h[:, h.cols].bitcast(F32), ALU.subtract
                                  ).then_inc(o_low, 1)

            def c_y1(h):
                dve.wait_ge(proj_ready, h.n())
                dve.wait_ge(x_res_set, h.loop.half(h.c).n())
                if h.follows(2):
                    dve.wait_ge(y2_ready, h.n(2))
                dve.tensor_tensor(y1[:, h.par, h.cols], c_banks(h)[0][:, h.cols], x_res[:, h.par, h.cols], ALU.add
                                  ).then_inc(y1_ready, 1)

            def c_stats(h):
                statistics(h, c_banks(h)[0], yT_ready, stats2, ln2_stats)
                aggregate(h, stats2, ln2_stats, mv2, ln2_mv, yn_tok_set)

            def c_norm(h):
                normalise(h, yn_tok, c_banks(h)[0], mv2, rstd2, ln2_rstd, yn_tok_set, ynT_ready)

            def c_yn(h):
                dve.wait_ge(yn_high, h.n())
                dve.tensor_tensor(yn_l[:, h.cols], c_banks(h)[0][:, h.cols], yn_h[:, h.cols].bitcast(F32), ALU.subtract
                                  ).then_inc(yn_low, 1)

            def c_y2(h):
                dve.wait_ge(fc2_ready, h.n())
                if h.follows(1):
                    dve.wait_ge(y2_low, h.n(1))
                dve.wait_ge(y1_ready, h.n())
                dve.scalar_tensor_tensor(y2[:, h.cols], c_banks(h)[1][:, h.cols], col(FC2B), y1[:, h.par, h.cols],
                                         ALU.add, ALU.add).then_inc(y2_ready, 1)

            def c_kv(h):
                dve.wait_ge(kv_ready, h.n())
                if h.follows(2):
                    dve.wait_ge(kvT_ready, h.of_parity(2))
                tiles = slice(h.tiles[0], h.tiles[-1] + 1)
                dve.tensor_tensor(kv_tok[:, h.par, tiles], c_banks(h)[1][:].rearrange("row (t e) -> row t e", t=4)[:, tiles],
                                  kv_bias[:].unsqueeze(1).to_broadcast([128, len(h.tiles), 2 * E]), ALU.add
                                  ).then_inc(kv_kept, 1)

            def d_kvT(loop, c):
                dve.wait_ge(kvT_ready, loop.image(c))
                dve.tensor_scalar(kvT[:], p_d[0:E, 0:E], 1.0 / TOKENS, None, ALU.mult).then_inc(kvT_kept, 1)

            def d_bT(loop, c):
                dve.wait_ge(bT_ready, loop.image(c))
                dve.tensor_copy(bT[:], p_d[0:E, 0:C]).then_inc(bT_kept, 1)

            def d_mT(loop, c):
                dve.wait_ge(mT_ready, loop.image(c))
                if loop.follows(c - 1):
                    dve.wait_ge(fin_ready[1], loop.image(c - 1))
                if loop.follows(c - 1):
                    dve.wait_ge(fin_kept[1], loop.image(c - 1))
                dve.tensor_tensor(mT[:], p_d[:, 0:C], ident[:], ALU.add).then_inc(mT_kept, 1)
                dve.tensor_tensor(d_col[:], p_d[:, C:C + 1], col(BO), ALU.add).then_inc(d_kept, 1)
                dve.wait_ge(mT_kept, loop.image(c))
                dve.tensor_copy(m_h[:], mT[:]).then_inc(m_high, 1)
                dve.wait_ge(m_high, loop.image(c))
                dve.tensor_tensor(m_l[:], mT[:], m_h[:].bitcast(F32), ALU.subtract).then_inc(m_low, 1)

            def hidden_low(h, t):
                dve.wait_ge(hid_high[t], h.n())
                dve.wait_ge(hid_full[t], h.n())
                dve.wait_ge(fc2_ready, h.n(1))
                dve.tensor_tensor(hid_l[:, t, h.cols], hid[:, t, h.cols], hid_h[:, t, h.cols].bitcast(F32), ALU.subtract
                                  ).then_inc(hid_low[t], 1)

            def d_out_last(loop):
                dve.wait_ge(fin_ready[1], loop.image(0))
                dve.wait_ge(out_dma[1], loop.image(-1, times=16))
                for v in range(2):
                    last = dve.tensor_scalar(in_rows(out_sb[:, 1, :], v), in_windows(p_a[0][:], v), d_col[:, 0:1],
                                             None, ALU.add)
                last.then_inc(fin_kept[1], 1)

            def prologue(loop):
                a = loop.half(0)
                a_stats(a)
                a_aggregate(a)
                load_qkv_weights()
                a_norm(a)
                load_qkv_biases()
                head_columns()
                a_xn(a)
                a_q(a)
                a_k(a)
                a_k_low_block(a)
                load_weights()
                a_stats(loop.half(1))
                a_aggregate(loop.half(1))
                load_biases()

            def step(loop, b, with_a, with_next, with_c, with_tail, with_d, with_last=False):
                a, next_a, c, tail = loop.half(b.c + 1), loop.half(b.c + 2), loop.half(b.c - 1), loop.half(b.c - 2)
                b_max(b, 0)
                b_widen(b, 0)
                if not with_c:
                    a_norm(a)
                if with_c:
                    c_o(c)
                b_max(b, 1)
                b_widen(b, 1)
                if with_c:
                    c_y1(c)
                b_max(b, 2)
                if with_a:
                    a_xn(a)
                if with_tail:
                    c_y2(tail)
                b_norm(b, 0)
                if not with_c:
                    split_weights()
                if with_c:
                    c_stats(c)
                if with_tail:
                    c_kv(tail)
                if with_a:
                    a_q(a)
                b_max(b, 3)
                if with_d:
                    d_kvT(loop, -1)
                if with_c:
                    c_norm(c)
                if with_a:
                    a_k(a)
                if with_d:
                    d_bT(loop, -1)
                b_norm(b, 1)
                b_widen(b, 3)
                if with_d:
                    d_mT(loop, -1)
                if with_next:
                    a_stats(next_a)
                if with_c:
                    c_yn(c)
                if with_next:
                    a_aggregate(next_a)
                if with_last:
                    c_o(Part(loop, 0))
                b_norm(b, 2)
                if with_a:
                    a_k_low_block(a)
                if with_last:
                    c_y1(Part(loop, 0))
                if with_next:
                    a_norm(next_a)
                b_norm(b, 3)

            def step_even(loop, more, c):
                step(loop, loop.half(0), True, more, c, c, False)

            def step_odd(loop, more, d):
                step(loop, loop.half(1), more, more, True, d, d, not more)

            def epilogue(loop):
                early, late = Part(loop, 0), Part(loop, 1)
                c_stats(early)
                c_o(late)
                c_norm(early)
                c_y1(late)
                c_yn(early)
                c_stats(late)
                c_y2(loop.half(0))
                c_norm(late)
                hidden_low(early, 0)
                hidden_low(early, 1)
                c_yn(late)
                c_kv(loop.half(0))
                c_y2(early)
                hidden_low(late, 0)
                hidden_low(late, 1)
                c_kv(early)
                c_y2(late)
                c_kv(late)
                d_kvT(loop, 0)
                d_bT(loop, 0)
                d_mT(loop, 0)
                d_out_last(loop)

            images(dve, prologue, step_even, step_odd, epilogue)


_INS = ['x', 'L0_conv_ln1_g', 'L0_conv_ln1_b', 'L0_conv_in_w', 'L0_conv_in_b', 'L0_conv_out_w', 'L0_conv_out_b',
        'L0_conv_ln2_g', 'L0_conv_ln2_b', 'L0_conv_fc1_w', 'L0_conv_fc1_b', 'L0_conv_fc2_w', 'L0_conv_fc2_b',
        'L1_conv_wq', 'L1_conv_bq', 'L1_conv_wk', 'L1_conv_bk', 'L1_conv_wv', 'L1_conv_bv', 'L1_conv_wo', 'L1_conv_bo']


def kernel(**inputs):
    import numpy as np
    import concourse.bacc as bacc
    from concourse.bass_utils import run_bass_kernel_spmd

    nc = bacc.Bacc("TRN2", target_bir_lowering=False, num_devices=1)
    arrays, args = {}, []
    for name in _INS:
        a = np.ascontiguousarray(inputs[name])
        arrays[f"in_{name}"] = a
        args.append(nc.dram_tensor(f"in_{name}", a.shape, mybir.dt.from_np(a.dtype), kind="ExternalInput").ap())
    args.append(nc.dram_tensor("out", (IMAGES, C, SIDE, SIDE), F32, kind="ExternalOutput").ap())
    build(nc, *args)
    result = run_bass_kernel_spmd(nc, [arrays], core_ids=[0])
    return result.results[0]["out"]
```
